# Optimizing a Trainium2 kernel written in Bass

```python
import numpy as np
import jax
import jax.numpy as jnp

def _softmax(x, axis=-1):
    return jax.nn.softmax(x, axis=axis)

def _gelu(x):
    return jax.nn.gelu(x, approximate=True)

def _silu(x):
    return jax.nn.silu(x)

def _sigmoid(x):
    return jax.nn.sigmoid(x)

def _layernorm(x, axis=-1, eps=1e-05):
    m = jnp.mean(x, axis=axis, keepdims=True)
    v = jnp.var(x, axis=axis, keepdims=True)
    return (x - m) / jnp.sqrt(v + eps)

def _scatter_add(tgt, idx, src, axis=0):
    return tgt.at[idx].add(src)

def _segment_sum(src, seg, n):
    return jax.ops.segment_sum(src, seg, n)
kernel_name = 'mk_perceiver_d1_seqx_r2_a6c956'

def setup_inputs(seed: int=0):
    np.random.seed(seed)
    _w = jnp.asarray

    def _rec_inputs():
        import jax
        import jax.numpy as jnp
        _rk = jax.random.key(seed)
        x = 4.136e-05 + 0.9999 * jax.random.normal(jax.random.fold_in(_rk, 1), (8, 64, 512), jnp.float32)
        _lenS = 64 - jax.random.randint(jax.random.fold_in(_rk, 7), (8,), 0, max(1, 64 // 4) + 1, jnp.int32)
        _lenS2 = 1601 - jax.random.randint(jax.random.fold_in(_rk, 8), (8,), 0, max(1, 1601 // 4) + 1, jnp.int32)
        _ctx_1024P = jax.random.normal(jax.random.fold_in(_rk, 11), (8, 16, 512), jnp.float32)
        _ctx_1024c = jax.random.dirichlet(jax.random.fold_in(_rk, 511), 0.3 * jnp.ones((16,), jnp.float32), (8, 1601))
        _ctx_1024t = jnp.einsum('bsk,bkd->bsd', _ctx_1024c, _ctx_1024P)
        _ctx_1024t = _ctx_1024t * jax.lax.rsqrt(jnp.mean(jnp.square(_ctx_1024t)) + 1e-12) * 0.953939
        ctx_1024 = 7.22013e-05 + 1.00017 * (_ctx_1024t + 0.3 * jax.random.normal(jax.random.fold_in(_rk, 611), (8, 1601, 512), jnp.float32))
        return (x, ctx_1024)
    x, ctx_1024 = _rec_inputs()

    def _L0_xattn_setup():
        import jax, jax.numpy as jnp
        import numpy as np
        D_MODEL = 512
        N_HEADS = 16
        D_HEAD = D_MODEL // N_HEADS
        LN_EPS = 1e-05

        def layer_norm(x, gamma, beta):
            mu = jnp.mean(x, axis=-1, keepdims=True)
            var = jnp.mean(jnp.square(x - mu), axis=-1, keepdims=True)
            return (x - mu) * jax.lax.rsqrt(var + LN_EPS) * gamma + beta
        key = jax.random.key(seed)
        ks = jax.random.split(key, 8)
        B, T = (4, 1024)
        s = 1.0 / np.sqrt(D_MODEL)
        return {'encoder_seq': jax.random.normal(ks[0], (B, T, D_MODEL), jnp.float32), 'decoder_seq': jax.random.normal(ks[1], (B, T, D_MODEL), jnp.float32), 'Wq': jax.random.normal(ks[2], (D_MODEL, D_MODEL), jnp.float32) * s, 'bq': jnp.zeros((D_MODEL,), jnp.float32), 'Wk': jax.random.normal(ks[3], (D_MODEL, D_MODEL), jnp.float32) * s, 'bk': jnp.zeros((D_MODEL,), jnp.float32), 'Wv': jax.random.normal(ks[4], (D_MODEL, D_MODEL), jnp.float32) * s, 'bv': jnp.zeros((D_MODEL,), jnp.float32), 'ln_gamma': jnp.ones((D_MODEL,), jnp.float32), 'ln_beta': jnp.zeros((D_MODEL,), jnp.float32)}
    _L0_xattn_all = _L0_xattn_setup()
    _L0_xattn_in = {k: v for k, v in _L0_xattn_all.items() if k in ('Wq', 'bq', 'Wk', 'bk', 'Wv', 'bv', 'ln_gamma', 'ln_beta')}
    del _L0_xattn_all

    def _L0_attn_setup():
        import jax, jax.numpy as jnp
        import numpy as np
        import math
        T, N, D, H = (1024, 2, 512, 16)
        HD = D // H
        key = jax.random.key(seed)
        k1, k2, k3, k4, k5 = jax.random.split(key, 5)
        scale = 0.02
        return {'x': jax.random.normal(k1, (T, N, D), dtype=jnp.float32), 'q_weight': jax.random.normal(k2, (D, H, HD), dtype=jnp.float32) * scale, 'v_weight': jax.random.normal(k3, (D, H, HD), dtype=jnp.float32) * scale, 'out_w': jax.random.normal(k4, (D, D), dtype=jnp.float32) * scale, 'out_b': jax.random.normal(k5, (D,), dtype=jnp.float32) * scale}
    _L0_attn_all = _L0_attn_setup()
    _L0_attn_in = {k: v for k, v in _L0_attn_all.items() if k in ('q_weight', 'v_weight', 'out_w', 'out_b')}
    del _L0_attn_all

    def _L0_ffn_setup():
        import jax, jax.numpy as jnp
        import numpy as np
        B, N, DIM = (2, 1024, 512)
        HEADS, DIM_HEAD, EXPERTS = (8, 64, 8)
        SCALE = DIM_HEAD ** (-0.5)
        key = jax.random.key(seed)
        ks = jax.random.split(key, 6)
        dim_inner = HEADS * DIM_HEAD
        return {'x': jax.random.normal(ks[0], (B, N, DIM), jnp.float32), 'w_q': jax.random.normal(ks[1], (DIM, dim_inner), jnp.float32) * 0.02, 'w_k': jax.random.normal(ks[2], (DIM, dim_inner), jnp.float32) * 0.02, 'w_gate': jax.random.normal(ks[3], (DIM, HEADS * EXPERTS), jnp.float32) * 0.02, 'value_experts': jax.random.normal(ks[4], (EXPERTS, HEADS, DIM, DIM_HEAD), jnp.float32) * 0.02, 'output_experts': jax.random.normal(ks[5], (EXPERTS, HEADS, DIM_HEAD, DIM), jnp.float32) * 0.02}
    _L0_ffn_all = _L0_ffn_setup()
    _L0_ffn_in = {k: v for k, v in _L0_ffn_all.items() if k in ('w_q', 'w_k', 'w_gate', 'value_experts', 'output_experts')}
    del _L0_ffn_all
    return {'x': x, 'ctx_1024': ctx_1024, 'L0_xattn_Wq': _L0_xattn_in['Wq'], 'L0_xattn_bq': _L0_xattn_in['bq'], 'L0_xattn_Wk': _L0_xattn_in['Wk'], 'L0_xattn_bk': _L0_xattn_in['bk'], 'L0_xattn_Wv': _L0_xattn_in['Wv'], 'L0_xattn_bv': _L0_xattn_in['bv'], 'L0_xattn_ln_gamma': _L0_xattn_in['ln_gamma'], 'L0_xattn_ln_beta': _L0_xattn_in['ln_beta'], 'L0_attn_q_weight': _L0_attn_in['q_weight'], 'L0_attn_v_weight': _L0_attn_in['v_weight'], 'L0_attn_out_w': _L0_attn_in['out_w'], 'L0_attn_out_b': _L0_attn_in['out_b'], 'L0_ffn_w_q': _L0_ffn_in['w_q'], 'L0_ffn_w_k': _L0_ffn_in['w_k'], 'L0_ffn_w_gate': _L0_ffn_in['w_gate'], 'L0_ffn_value_experts': _L0_ffn_in['value_experts'], 'L0_ffn_output_experts': _L0_ffn_in['output_experts']}

def reference(x, ctx_1024, L0_xattn_Wq, L0_xattn_bq, L0_xattn_Wk, L0_xattn_bk, L0_xattn_Wv, L0_xattn_bv, L0_xattn_ln_gamma, L0_xattn_ln_beta, L0_attn_q_weight, L0_attn_v_weight, L0_attn_out_w, L0_attn_out_b, L0_ffn_w_q, L0_ffn_w_k, L0_ffn_w_gate, L0_ffn_value_experts, L0_ffn_output_experts):
    import jax
    import jax.numpy as jnp

    def _L0_xattn_ref(encoder_seq, decoder_seq, Wq, bq, Wk, bk, Wv, bv, ln_gamma, ln_beta):
        import jax, jax.numpy as jnp
        import numpy as np
        D_MODEL = 512
        N_HEADS = 16
        D_HEAD = D_MODEL // N_HEADS
        LN_EPS = 1e-05

        def layer_norm(x, gamma, beta):
            mu = jnp.mean(x, axis=-1, keepdims=True)
            var = jnp.mean(jnp.square(x - mu), axis=-1, keepdims=True)
            return (x - mu) * jax.lax.rsqrt(var + LN_EPS) * gamma + beta
        B, T_dec, _ = decoder_seq.shape
        T_enc = encoder_seq.shape[1]
        q = (decoder_seq @ Wq.T + bq).reshape(B, T_dec, N_HEADS, D_HEAD)
        k = (encoder_seq @ Wk.T + bk).reshape(B, T_enc, N_HEADS, D_HEAD)
        v = (encoder_seq @ Wv.T + bv).reshape(B, T_enc, N_HEADS, D_HEAD)
        scale = 1.0 / np.sqrt(D_HEAD)
        kv = jnp.einsum('bthd,bthe->bhde', k, v)
        att = jnp.einsum('bqhd,bhde->bqhe', q, kv) * scale
        att = att.reshape(B, T_dec, D_MODEL)
        return layer_norm(att + decoder_seq, ln_gamma, ln_beta)

    def _L0_attn_ref(x, q_weight, v_weight, out_w, out_b):
        import jax, jax.numpy as jnp
        import numpy as np
        import math
        T, N, D, H = (1024, 2, 512, 16)
        HD = D // H
        head_dim = q_weight.shape[-1]
        inv_sqrt_d = 1.0 / math.sqrt(head_dim)
        q = jnp.einsum('tbm,mhd->tbhd', x, q_weight)
        q_sq = jnp.einsum('tbhd,tbhd->tbh', q, q)
        squared_dist = q_sq[:, None] + q_sq[None, :] - 2.0 * jnp.einsum('tbhd,sbhd->tsbh', q, q)
        attn_logits = -squared_dist * inv_sqrt_d
        attn_weights = jax.nn.softmax(attn_logits, axis=1)
        A = jnp.einsum('mhd,nhd->hmn', q_weight, q_weight) * inv_sqrt_d
        XA = jnp.einsum('tbm,hmn->tbhn', x, A)
        PXA = jnp.einsum('tsbh,sbhm->tbhm', attn_weights, XA)
        PXAV = jnp.einsum('tbhm,mhd->tbhd', PXA, v_weight).reshape(x.shape[0], x.shape[1], -1)
        return PXAV @ out_w.T + out_b

    def _L0_ffn_ref(x, w_q, w_k, w_gate, value_experts, output_experts):
        import jax, jax.numpy as jnp
        import numpy as np
        B, N, DIM = (2, 1024, 512)
        HEADS, DIM_HEAD, EXPERTS = (8, 64, 8)
        SCALE = DIM_HEAD ** (-0.5)
        b, n, _ = x.shape
        q = (x @ w_q).reshape(b, n, HEADS, DIM_HEAD).transpose(0, 2, 1, 3)
        k = (x @ w_k).reshape(b, n, HEADS, DIM_HEAD).transpose(0, 2, 1, 3)
        gates = jax.nn.sigmoid((x @ w_gate).reshape(b, n, HEADS, EXPERTS).transpose(0, 2, 1, 3))
        sel = jnp.argmax(gates, axis=-1)
        gm = jax.nn.one_hot(sel, EXPERTS, dtype=x.dtype) * gates
        values = jnp.einsum('bhne,ehdk,bnd->bhnk', gm, value_experts, x)
        sim = jnp.einsum('bhid,bhjd->bhij', q * SCALE, k)
        causal_mask = jnp.triu(jnp.ones((n, n), dtype=bool), 1)
        sim = jnp.where(causal_mask, jnp.finfo(sim.dtype).min, sim)
        attn = jax.nn.softmax(sim, axis=-1)
        out = jnp.einsum('bhij,bhjk->bhik', attn, values)
        out = jnp.einsum('bhne,ehkd,bhnk->bhnd', gm, output_experts, out)
        return out.sum(axis=1)
    x = x + _L0_xattn_ref(ctx_1024, _layernorm(x, axis=-1), L0_xattn_Wq, L0_xattn_bq, L0_xattn_Wk, L0_xattn_bk, L0_xattn_Wv, L0_xattn_bv, L0_xattn_ln_gamma, L0_xattn_ln_beta)
    x = x + _L0_attn_ref(_layernorm(x, axis=-1), L0_attn_q_weight, L0_attn_v_weight, L0_attn_out_w, L0_attn_out_b)
    x = x + _L0_ffn_ref(_layernorm(x, axis=-1), L0_ffn_w_q, L0_ffn_w_k, L0_ffn_w_gate, L0_ffn_value_experts, L0_ffn_output_experts)
    return x

_drawn_inputs = setup_inputs


def setup_inputs(seed=0):
    import zlib

    import numpy as np

    out = dict(_drawn_inputs(seed))
    spreads = {'L0_xattn_bq': (0.0, 0.1),
     'L0_xattn_bk': (0.0, 0.1),
     'L0_xattn_bv': (0.0, 0.1),
     'L0_xattn_ln_gamma': (1.0, 0.2),
     'L0_xattn_ln_beta': (0.0, 0.1)}
    factors = {'L0_attn_q_weight': 8.0,
     'L0_attn_v_weight': 8.0,
     'L0_attn_out_w': 8.0,
     'L0_attn_out_b': 4.072,
     'L0_ffn_w_q': 8.0,
     'L0_ffn_w_k': 8.0,
     'L0_ffn_w_gate': 3.319,
     'L0_ffn_value_experts': 3.273,
     'L0_ffn_output_experts': 3.242}
    for name, (base, spread) in spreads.items():
        noise = np.random.default_rng([zlib.crc32(name.encode()), seed]).standard_normal(out[name].shape)
        drawn = base * np.exp(spread * noise) if base else spread * noise
        out[name] = jnp.asarray(drawn.astype(out[name].dtype))
    for name, factor in factors.items():
        out[name] = (out[name] * factor).astype(out[name].dtype)
    return out
```

```python
from contextlib import ExitStack
from math import sqrt

import concourse.bass as bass
from concourse import mybir

F32 = mybir.dt.float32
F32R = mybir.dt.float32r
BF16 = mybir.dt.bfloat16
ALU = mybir.AluOpType
ACT = mybir.ActivationFunctionType
AX_X = mybir.AxisListType.X

P = 128
MASKED = -1e30
LN_EPS = 1e-5


def perceiver_block(nc, a, out):
    B, S, D = a["x"].shape
    T = a["ctx_1024"].shape[1]
    N = B * S
    KC = D // P
    NT = N // P
    ROWS = 4
    CH = T // (P * ROWS)
    REM = T - CH * P * ROWS
    NSLOT = CH * ROWS + 1
    H1 = 16
    D1 = D // H1
    H2 = 8
    D2 = D // H2
    NE = 8
    NG = S // 16
    INV1 = 1.0 / sqrt(D1)
    SCALE2 = float(D2) ** -0.5
    NADD = NSLOT - 1
    SUMMED = [ROWS * c + ROWS - 1 for c in range(CH)] + [NADD]
    assert (N, D, KC, NT, CH, NG) == (512, 512, 4, 4, 3, 4) and 0 < REM < P

    with ExitStack() as ctx:
        def sb(name, shape, dt=F32):
            return ctx.enter_context(nc.sbuf_tensor(name, shape, dt))

        def sem(name):
            return ctx.enter_context(nc.semaphore(name))

        raw = sb("raw", [P, NSLOT, D])
        hi = sb("hi", [P, NSLOT, D], F32R)
        lo = sb("lo", [P, NSLOT, D], F32R)
        xres = sb("xres", [P, NT, D])
        xn = sb("xn", [P, NT, D])
        qT = sb("qT", [P, KC, N])
        g32 = sb("g32", [P, KC, D])
        mb = sb("mb", [P, KC, D])
        wk = sb("wk", [P, KC, D])
        kv = sb("kv", [P, B, D])
        sx = sb("sx", [P, B, D])
        wvh = sb("wvh", [P, KC, D], F32R)
        wvl = sb("wvl", [P, KC, D], F32R)
        gh = sb("gh", [P, KC, D], F32R)
        gl = sb("gl", [P, KC, D], F32R)
        gamma = sb("gamma", [P, D])
        beta = sb("beta", [P, D])
        out_b = sb("out_b", [P, D])
        bv8 = sb("bv8", [B, D])
        psum_tmp = sb("psum_tmp", [P, D])
        bq = sb("bq", [P, KC])
        ident = sb("ident", [P, P])
        identb = sb("identb", [P, P], BF16)
        headmask = sb("headmask", [P, P])
        posmask = sb("posmask", [P, 4 * P], BF16)
        causal = sb("causal", [P, 4 * P], BF16)
        neghalf = sb("neghalf", [P, P], F32R)
        cb = sb("cb", [P, KC, P])
        scol = sb("scol", [P, KC, B])
        ones = sb("ones", [P, 1])
        expo = sb("expo", [P, NT])
        stats = sb("stats", [P, NT, 6])
        mv = sb("mv", [P, NT, 2])
        vareps = sb("vareps", [P, NT])
        rstd = sb("rstd", [P, NT])
        negmax = sb("negmax", [P, 2, 4])
        rz = sb("rz", [P, 2, 4])

        a2 = sx[0:2, :, :]
        b2 = raw[0:2, 4:12, :]
        rk = raw[0:B, 12, :]
        rv = psum_tmp[0:B, :]
        tmp = raw[:, 9:11, :]
        wg_raw = raw[:, 8, :].rearrange("p (k n) -> p k n", n=P)
        wg_hi = hi[:, 8, :].rearrange("p (k n) -> p k n", n=P)
        wg_lo = lo[:, 8, :].rearrange("p (k n) -> p k n", n=P)
        sxf = sx[:, :, :].rearrange("p b d -> p (b d)")
        vv = sxf[:, 0:NG * H1 * (D1 + 1)].rearrange("p (g h e) -> p g h e", g=NG, h=H1)
        vals = sxf[:, 0:NT * H2 * (D2 + 1)].rearrange("p (i h e) -> p i h e", i=NT, h=H2)
        ering = sxf[:, 2112:2112 + 2 * D].rearrange("p (r n) -> p r n", r=2)
        gateT = sxf[:, 3136:3136 + N]
        gsc = raw[:, 11, :].rearrange("p (r n) -> p r n", r=2)
        gates = gsc[:, 0, :]
        gsel = gsc[:, 1, :]
        gm = sxf[:, 3648:3648 + NT * H2 * NE]
        tie = sb("tie", [P, NT * H2 * NE])
        gmax = sb("gmax", [P, NT * H2])

        bank = [ctx.enter_context(nc.psum_tensor(f"bank{n}", [P, 512], F32)) for n in range(8)]

        ld_x, ld_qv, ld_wq, ld_wv, ld_wk, ld_par = (sem(s) for s in ("ld_x", "ld_qv", "ld_wq", "ld_wv", "ld_wk", "ld_par"))
        ld_ctx = [sem(f"ld_ctx{c}") for c in range(CH + 1)]
        ld_wv2, ld_rows, ld_bvrow, ld_wg = (sem(s) for s in ("ld_wv2", "ld_rows", "ld_bvrow", "ld_wg"))
        ld_w = [sem("ld_w0"), sem("ld_w1")]
        consts, bfconst = sem("consts"), sem("bfconst")
        c_mm, c_done = sem("c_mm"), sem("c_done")
        s_stats, s_aggr, s_var, s_rstd, s_norm = (sem(s) for s in ("s_stats", "s_aggr", "s_var", "s_rstd", "s_norm"))
        xT_mm, xT_hi, xT_lo = sem("xT_mm"), sem("xT_hi"), sem("xT_lo")
        w_hi, w_lo = sem("w_hi"), sem("w_lo")
        q_mm, q_done = sem("q_mm"), sem("q_done")
        ctx_hi, ctx_lo, ctx_sum, sum_out = (sem(s) for s in ("ctx_hi", "ctx_lo", "ctx_sum", "sum_out"))
        gram_mm, g_act, g_dve, gt_mm, gh_done, gl_done = (sem(s) for s in ("gram_mm", "g_act", "g_dve", "gt_mm", "gh_done", "gl_done"))
        m_mm, m_done, kv_mm, kv_done = (sem(s) for s in ("m_mm", "m_done", "kv_mm", "kv_done"))
        s_mm, s_done, r_mm, rk_done, rv_done, r2_mm, r2_tmp, r2_done = (
            sem(s) for s in ("s_mm", "s_done", "r_mm", "rk_done", "rv_done", "r2_mm", "r2_tmp", "r2_done"))
        att_mm, y_done, xb_done, z_done, x1_done, ob_done = (
            sem(s) for s in ("att_mm", "y_done", "xb_done", "z_done", "x1_done", "ob_done"))
        qq_done, qq_hi, qq_lo, vv_mm, vv_done, vv_one = (sem(s) for s in ("qq_done", "qq_hi", "qq_lo", "vv_mm", "vv_done", "vv_one"))
        lg_mm, mx_done, nm_done, e_done, eT_mm, eT_done, pv_mm, rz_done, pv_done = (
            sem(s) for s in ("lg_mm", "mx_done", "nm_done", "e_done", "eT_mm", "eT_done", "pv_mm", "rz_done", "pv_done"))
        pT_mm, pT_hi, pT_lo, op_mm, x2_done = (sem(s) for s in ("pT_mm", "pT_hi", "pT_lo", "op_mm", "x2_done"))
        k_done, wg_hi_done, wg_lo_done, gl_mm, gT_done, gl2_mm, ge_done, g_step, gm_done = (
            sem(s) for s in ("k_done", "wg_hi_done", "wg_lo_done", "gl_mm", "gT_done", "gl2_mm", "ge_done", "g_step", "gm_done"))
        v_zero, v_mm, v_gated, v_added = (sem(s) for s in ("v_zero", "v_mm", "v_gated", "v_added"))
        og_done, oT_mm, oT_hi, oT_lo, out_mm, fin, st_out = (
            sem(s) for s in ("og_done", "oT_mm", "oT_hi", "oT_lo", "out_mm", "fin", "st_out"))

        block = ctx.enter_context(nc.Block())

        W_Q1, W_OUT, W_Q2, W_K2, W_VE, W_OE = 0, 1, 2, 3, 4, 4 + NE
        w_fixed = [a["qw"], a["owT"], a["wq2"], a["wk2"]]

        def blocks(w):
            return w.rearrange("(k p) n -> p k n", p=P)

        def half(h):
            return slice(4 * h, 4 * h + 4)

        def chunk(c):
            return (slice(ROWS * c, ROWS * c + ROWS), P) if c < CH else (slice(CH * ROWS, CH * ROWS + 1), REM)

        def gram_cols(m):
            return min(m, KC - 2) * P

        def three(pe, dst, wh, wl, xh, xl, first, last):
            pe.matmul(dst, wh, xh, start=first, stop=False)
            pe.matmul(dst, wh, xl, start=False, stop=False)
            return pe.matmul(dst, wl, xh, start=False, stop=last)

        @block.sync
        def _(sp):
            sp.dma_start(xres[:, :, :], a["x"].rearrange("b s d -> (b s) d").rearrange("(i p) d -> p i d", p=P)).then_inc(ld_x, 16)
            sp.dma_start(raw[:, half(0), :], blocks(a["qw"])).then_inc(ld_qv, 16)
            sp.dma_start(g32[:, :, :], blocks(a["vw"])).then_inc(ld_qv, 16)
            sp.dma_start(raw[:, half(1), :], blocks(a["WqT"])).then_inc(ld_wq, 16)
            sp.dma_start(bq[:, :], a["bq"].rearrange("(k p) -> p k", p=P), allow_slow_non_contiguous=True).then_inc(ld_par, 16)
            sp.dma_start(raw[:, half(2), :], blocks(a["WvT"])).then_inc(ld_wv, 16)
            for t, name in ((gamma, "gamma"), (beta, "beta"), (out_b, "out_b")):
                sp.dma_start(t[:, :], a[name].rearrange("(o d) -> o d", o=1).broadcast_to([P, D])).then_inc(ld_par, 16)
            sp.dma_start(bv8[:, :], a["bv"].rearrange("(o d) -> o d", o=1).broadcast_to([B, D])).then_inc(ld_par, 16)
            sp.dma_start(wk[:, :, :], blocks(a["WkT"])).then_inc(ld_wk, 16)

            def load_ctx(b, c):
                r, k = chunk(c)
                if c < CH:
                    src = a["ctx_1024"][b, c * P * ROWS:(c + 1) * P * ROWS, :].rearrange("(p r) d -> p r d", r=ROWS)
                else:
                    src = a["ctx_1024"][b, CH * P * ROWS:T, :].rearrange("p (r d) -> p r d", r=1)
                sp.dma_start(raw[0:k, r, :], src).then_inc(ld_ctx[c], 16)

            load_ctx(0, 3)
            sp.wait_ge(c_mm, 1)
            load_ctx(0, 0)
            sp.wait_ge(w_lo, 1)
            load_ctx(0, 1)
            sp.wait_ge(w_lo, 2)
            load_ctx(0, 2)
            with sp.Fori(1, B) as b:
                for c in range(CH + 1):
                    sp.wait_ge(ctx_sum, b * NADD + (SUMMED[c] - NADD))
                    load_ctx(b, c)
            sp.wait_ge(gh_done, 5 * B)
            sp.wait_ge(gl_done, 5 * B)
            sp.wait_ge(gt_mm, B)
            sp.dma_start(g32[:, :, :], blocks(a["WvT"])).then_inc(ld_wv2, 16)
            sp.wait_ge(ctx_lo, 4 * B)
            sp.wait_ge(ctx_sum, NADD * B)
            row = lambda name: a[name].rearrange("(o d) -> o d", o=1).unsqueeze(1).broadcast_to([1, B, D])
            sp.dma_start(b2[0:1, :, :], row("bv")).then_inc(ld_bvrow, 16)
            sp.dma_start(raw[:, half(0), :], blocks(a["qw"])).then_inc(ld_w[0], 16)
            sp.wait_ge(s_mm, 1)
            sp.dma_start(a2[1:2, :, :], row("bk")).then_inc(ld_rows, 16)
            sp.wait_ge(rk_done, 1)
            sp.dma_start(a2[0:1, :, :], rk).then_inc(ld_rows, 16)
            sp.wait_ge(rv_done, 1)
            sp.dma_start(b2[1:2, :, :], rv).then_inc(ld_rows, 16)
            sp.wait_ge(r2_mm, B)
            sp.dma_start(raw[:, half(1), :], blocks(a["owT"])).then_inc(ld_w[1], 16)
            sp.wait_ge(wg_hi_done, 1)
            sp.dma_start(wg_raw[:, :, 0:H2 * NE], blocks(a["wg"])).then_inc(ld_wg, 16)
            sp.wait_ge(w_lo, 3)
            sp.dma_start(raw[:, half(0), :], blocks(a["wq2"])).then_inc(ld_w[0], 16)
            sp.wait_ge(w_lo, 4)
            sp.dma_start(raw[:, half(1), :], blocks(a["wk2"])).then_inc(ld_w[1], 16)
            for s in range(2):
                sp.wait_ge(w_lo, 5 + s)
                sp.dma_start(raw[:, half(s), :], blocks(a["ve"][s])).then_inc(ld_w[s], 16)
            with sp.Fori(1, NE // 2) as j:
                for s in range(2):
                    sp.wait_ge(w_lo, j * 2 + 5 + s)
                    sp.dma_start(raw[:, half(s), :], blocks(a["ve"][j * 2 + s])).then_inc(ld_w[s], 16)
            with sp.Fori(0, NE // 2) as j:
                for s in range(2):
                    sp.wait_ge(w_lo, j * 2 + 5 + NE + s)
                    sp.dma_start(raw[:, half(s), :], blocks(a["oe"][j * 2 + s])).then_inc(ld_w[s], 16)
            outv = out.rearrange("b s d -> (b s) d").rearrange("(i p) d -> p i d", p=P)
            for i in range(NT):
                sp.wait_ge(fin, i + 1)
                sp.dma_start(outv[:, i, :], xres[:, i, :]).then_inc(st_out, 16)
            sp.wait_ge(st_out, 16 * NT)

        @block.gpsimd
        def _(pool):
            pool.memset(ident[:, :], 0.0).then_inc(consts, 1)
            pool.memset(identb[:, :], 0.0).then_inc(consts, 1)
            pool.memset(headmask[:, :], 1.0).then_inc(consts, 1)
            pool.memset(posmask[:, :], MASKED).then_inc(consts, 1)
            pool.memset(causal[:, :], 0.0).then_inc(consts, 1)
            pool.memset(ones[:, :], 1.0).then_inc(consts, 1)
            pool.memset(expo[:, :], -0.5).then_inc(consts, 1)
            pool.memset(neghalf[:, :].bitcast(F32), -0.5).then_inc(consts, 1)
            tie4 = tie[:, :].rearrange("p (g e) -> p g e", e=NE)
            for e in range(NE):
                pool.memset(tie4[:, :, e], float(NE - e)).then_inc(consts, 1)
            pool.wait_ge(consts, 8 + NE)
            for m in (ident, identb):
                pool.affine_select(out=m[:, :], in_=m[:, :], compare_op=ALU.not_equal, fill=1.0, base=0,
                                   pattern=[[-1, P]], channel_multiplier=1).then_inc(consts, 1)
            hm = headmask[:, :].rearrange("p (h d) -> p h d", d=D1)
            pool.affine_select(out=hm, in_=hm, compare_op=ALU.is_ge, fill=0.0, base=0,
                               pattern=[[-D1, 4], [0, D1]], channel_multiplier=1).then_inc(consts, 1)
            pool.wait_ge(consts, 11 + NE)
            pool.affine_select(out=hm, in_=hm, compare_op=ALU.is_ge, fill=0.0, base=D1 - 1,
                               pattern=[[D1, 4], [0, D1]], channel_multiplier=-1).then_inc(consts, 1)

            def rstd_of(n):
                pool.wait_ge(s_var, n)
                pool.tensor_tensor(rstd[:, :], vareps[:, :], expo[:, :], ALU.pow).then_inc(s_rstd, 1)

            rstd_of(1)

            pm = posmask[:, :].rearrange("p (s q) -> p s q", q=16)
            for t in range(P // 16):
                for k in ((-1, 1) if t else (1,)):
                    n = 2 * t - (1 if k < 0 else 0)
                    if n:
                        pool.wait_ge(bfconst, n)
                    pool.affine_select(out=pm, in_=pm, compare_op=ALU.not_equal, fill=0.0, base=-16 * t * k,
                                       pattern=[[0, 4 * P // 16], [-1, 16]], channel_multiplier=1).then_inc(bfconst, 1)
            n0 = 2 * (P // 16) - 1
            cz = causal[:, :].rearrange("p (r b j) -> p r b j", r=4, b=2)
            pool.affine_select(out=cz[:, :, 1, :], in_=cz[:, :, 1, :], compare_op=ALU.is_ge, fill=MASKED, base=-S,
                               pattern=[[0, 4], [-1, S]], channel_multiplier=1).then_inc(bfconst, 1)
            pool.affine_select(out=cz[:, :, 0, :], in_=cz[:, :, 0, :], compare_op=ALU.is_ge, fill=MASKED, base=0,
                               pattern=[[0, 4], [-1, S]], channel_multiplier=1).then_inc(bfconst, 1)
            pool.wait_ge(bfconst, n0 + 2)
            pool.affine_select(out=cz[:, :, 0, :], in_=cz[:, :, 0, :], compare_op=ALU.is_ge, fill=MASKED, base=S - 1,
                               pattern=[[0, 4], [0, S]], channel_multiplier=-1).then_inc(bfconst, 1)

            pool.wait_ge(s_norm, NT)
            pool.wait_ge(ld_par, 80)
            for i in range(NT):
                pool.tensor_tensor(xres[:, i, :], xres[:, i, :], beta[:, :], ALU.add).then_inc(xb_done, 1)

            def sums(b, first):
                n = 0
                for t in range(1, NSLOT):
                    c, k = (t // ROWS, P) if t < CH * ROWS else (CH, REM)
                    if t % ROWS == 0 or t == 1:
                        pool.wait_ge(ld_ctx[c], b * 16 + 16)
                    if t > 1:
                        pool.wait_ge(ctx_sum, b * NADD + n)
                    elif not first:
                        pool.wait_ge(sum_out, b)
                    if t in SUMMED:
                        pool.wait_ge(ctx_lo, b * 4 + c + 1)
                    pool.tensor_tensor(psum_tmp[0:k, :], (raw[:, 0, :] if t == 1 else psum_tmp[0:k, :]), raw[0:k, t, :],
                                       ALU.add).then_inc(ctx_sum, 1)
                    n += 1

            sums(0, True)
            with pool.Fori(1, B) as b:
                sums(b, False)

            rstd_of(2)
            rstd_of(3)
            pool.wait_ge(x1_done, NT)
            pool.wait_ge(s_norm, 3 * NT)
            for i in range(NT):
                pool.tensor_tensor(xres[:, i, :], xres[:, i, :], out_b[:, :], ALU.add).then_inc(ob_done, 1)
            pool.wait_ge(r2_mm, B)
            pool.memset(vv[:, :, :, D1:D1 + 1], 1.0).then_inc(vv_one, 1)
            pool.wait_ge(r2_mm, B)
            pool.wait_ge(ld_rows, 48)
            pool.memset(wg_raw[:, :, H2 * NE:P], 0.0).then_inc(wg_hi_done, 1)
            rstd_of(4)
            pool.wait_ge(pv_mm, H1)
            pool.memset(vals[:, :, :, :], 0.0).then_inc(v_zero, 1)
            pool.wait_ge(v_zero, 1)
            pool.memset(vals[:, :, :, D2:D2 + 1], 1.0).then_inc(v_zero, 1)

            def add_values(e):
                for i in range(NT):
                    pool.wait_ge(v_gated, e * NT + i + 1)
                    v = vals[:, i, :, 0:D2]
                    pool.tensor_tensor(v, v, tmp[:, i % 2, :].rearrange("p (h k) -> p h k", k=D2), ALU.add).then_inc(v_added, 1)

            with pool.Fori(0, NE) as e:
                add_values(e)

        @block.scalar
        def _(act):
            def xT_high(n):
                for k in range(KC):
                    act.wait_ge(xT_mm, KC * n + k + 1)
                    act.activation(gh[:, k, :], bank[k][:, :], ACT.Copy).then_inc(xT_hi, 1)

            act.wait_ge(ld_wq, 16)
            act.activation(hi[:, half(1), :], raw[:, half(1), :], ACT.Copy).then_inc(w_hi, 1)
            act.wait_ge(ld_wv, 16)
            act.activation(wvh[:, :, :], raw[:, half(2), :], ACT.Copy).then_inc(w_hi, 1)
            xT_high(0)

            def ctx_high(b, c, first):
                r, k = chunk(c)
                act.wait_ge(ld_ctx[c], b * 16 + 16)
                if not first:
                    act.wait_ge(gram_mm, b * 4 + c - 3)
                act.activation(hi[0:k, r, :], raw[0:k, r, :], ACT.Copy).then_inc(ctx_hi, 1)

            def g_high(b, first):
                act.wait_ge(gram_mm, b * 4 + 4)
                if not first:
                    act.wait_ge(gl_done, b * 5)
                    act.wait_ge(gt_mm, b)
                act.activation(g32[:, 0, :], bank[0][:, :], ACT.Copy).then_inc(g_act, 1)
                act.activation(g32[:, 1, P:D], bank[1][:, P:D], ACT.Copy).then_inc(g_act, 1)

            def gh_high(b, first):
                if first:
                    act.wait_ge(q_mm, KC)
                else:
                    act.wait_ge(m_mm, b * 4)
                act.wait_ge(g_act, b * 2 + 2)
                act.wait_ge(g_dve, b + 1)
                act.activation(gh[:, 0, :], g32[:, 0, :], ACT.Copy).then_inc(gh_done, 1)
                act.activation(gh[:, 1, P:D], g32[:, 1, P:D], ACT.Copy).then_inc(gh_done, 1)
                act.activation(gh[:, 2:4, 2 * P:D], g32[:, 2:4, 2 * P:D], ACT.Copy).then_inc(gh_done, 1)
                act.wait_ge(gt_mm, b + 1)
                act.activation(gh[:, 1:4, 0:P], bank[3][:, 0:3 * P].rearrange("p (m n) -> p m n", n=P), ACT.Copy).then_inc(gh_done, 1)
                act.activation(gh[:, 2:4, P:2 * P], bank[4][:, 0:2 * P].rearrange("p (m n) -> p m n", n=P), ACT.Copy).then_inc(gh_done, 1)

            def m_copy(b):
                for m in range(KC):
                    act.wait_ge(m_mm, b * 4 + m + 1)
                    act.activation(mb[:, m, :], bank[5 + m % 2][:, :], ACT.Copy).then_inc(m_done, 1)

            ctx_high(0, 0, True)
            for c in range(1, 4):
                if c == 1:
                    act.wait_ge(q_mm, KC)
                ctx_high(0, c, True)
            g_high(0, True)
            ctx_high(1, 0, False)
            gh_high(0, True)
            with act.Fori(1, B - 1) as b:
                for c in range(1, 4):
                    ctx_high(b, c, False)
                g_high(b, False)
                ctx_high(b + 1, 0, False)
                m_copy(b - 1)
                gh_high(b, False)
            for c in range(1, 4):
                ctx_high(B - 1, c, False)
            g_high(B - 1, False)
            m_copy(B - 2)
            gh_high(B - 1, False)
            m_copy(B - 1)

            act.wait_ge(s_mm, 1)
            act.activation(scol[:, :, :], bank[0][:, 0:KC * B].rearrange("p (k b) -> p k b", b=B), ACT.Copy).then_inc(s_done, 1)
            act.wait_ge(r_mm, 1)
            act.activation(rk, bank[1][0:B, :], ACT.Copy).then_inc(rk_done, 1)

            def w_high(n, slot, count):
                act.wait_ge(ld_w[slot], 16 * count)
                act.activation(hi[:, half(slot), :], raw[:, half(slot), :], ACT.Copy).then_inc(w_hi, 1)

            w_high(W_Q1, 0, 1)
            w_high(W_OUT, 1, 1)
            xT_high(1)

            def regroup(t):
                return t.rearrange("p (g t q) -> p t g q", t=P // 16, q=16)

            for k in range(KC):
                act.wait_ge(q_mm, KC + k + 1)
                act.activation(regroup(qT[:, k, :]), bank[4 + k][:, :].rearrange("p (t g q) -> p t g q", g=NG, q=16),
                               ACT.Copy).then_inc(q_done, 1)
            for k in range(KC):
                act.wait_ge(q_done, KC + k + 1)
                act.activation(xn[:, k, :], qT[:, k, :], ACT.Square).then_inc(qq_done, 1)
            for k in range(KC):
                act.wait_ge(qq_done, k + 1)
                act.activation(wvh[:, k, :], xn[:, k, :], ACT.Copy).then_inc(qq_hi, 1)
            for g in range(NG):
                act.wait_ge(vv_mm, g + 1)
                act.activation(vv[:, g, :, 0:D1], bank[g][:, :].rearrange("p (h e) -> p h e", e=D1), ACT.Copy).then_inc(vv_done, 1)

            def exps(u, scale):
                act.wait_ge(nm_done, u + 1)
                if u >= 2:
                    act.wait_ge(eT_mm, u - 1)
                for s in range(4):
                    act.activation(ering[:, u % 2, s * P:(s + 1) * P], bank[u % 2][:, s * P:(s + 1) * P], ACT.Exp,
                                   bias=negmax[:, u % 2, s:s + 1], scale=scale).then_inc(e_done, 1)

            for u in range(H1):
                exps(u, 2.0 * INV1)
            w_high(W_Q2, 0, 2)
            for k in range(KC):
                act.wait_ge(pT_mm, k + 1)
                act.activation(wvh[:, k, :].rearrange("p (t g q) -> p g t q", g=NG, q=16),
                               bank[k][:, :].rearrange("p (g t q) -> p g t q", g=NG, q=16), ACT.Copy).then_inc(pT_hi, 1)
            act.wait_ge(op_mm, NT)
            w_high(W_K2, 1, 2)
            act.wait_ge(ld_wg, 16)
            act.wait_ge(wg_hi_done, 1)
            act.activation(wg_hi, wg_raw, ACT.Copy).then_inc(wg_hi_done, 1)
            xT_high(2)
            for k in range(KC):
                act.wait_ge(q_mm, 2 * KC + k + 1)
                act.activation(qT[:, k, :], bank[4 + k][:, :], ACT.Copy, scale=SCALE2).then_inc(q_done, 1)
            act.wait_ge(gl_mm, 1)
            act.activation(gateT[0:H2 * NE, :], bank[4][0:H2 * NE, :], ACT.Copy).then_inc(gT_done, 1)
            act.wait_ge(gl2_mm, 1)
            act.activation(gates, bank[5][:, 0:NT * H2 * NE], ACT.Exp, scale=-1.0).then_inc(ge_done, 1)
            w_high(W_VE, 0, 3)
            for u in range(H1, H1 + 8):
                exps(u, 1.0)
            w_high(W_VE + 1, 1, 3)

            def expert_high(slot, count, used):
                act.wait_ge(ld_w[slot], count)
                act.wait_ge(used[0], used[1])
                act.activation(hi[:, half(slot), :], raw[:, half(slot), :], ACT.Copy).then_inc(w_hi, 1)

            with act.Fori(1, NE // 2) as j:
                for s in range(2):
                    expert_high(s, j * 16 + 48, (v_mm, (j * 2 + s) * NT - 4))
            for s in range(2):
                expert_high(s, 16 * (3 + NE // 2), (v_mm, (NE - 1 + s) * NT))

            def oT_high(e, buf):
                for k in range(KC):
                    act.wait_ge(oT_mm, e * 4 + k + 1)
                    act.activation(buf[:, k, :], bank[4 + k][:, :], ACT.Copy).then_inc(oT_hi, 1)

            oT_high(0, wvh)
            oT_high(1, gh)
            with act.Fori(0, NE // 2 - 1) as j:
                e = j * 2 + 1
                for s, buf in ((0, wvh), (1, gh)):
                    act.wait_ge(out_mm, e + s)
                    act.wait_ge(ld_w[s], e * 8 + 120)
                    act.activation(hi[:, half(s), :], raw[:, half(s), :], ACT.Copy).then_inc(w_hi, 1)
                    oT_high(e + (s + 1), buf)

        @block.tensor
        def _(pe):
            pe.wait_ge(ld_qv, 32)
            for c in range(KC):
                for k in range(KC):
                    cols = slice(c * P, (c + 1) * P)
                    mm = pe.matmul(bank[7][:, cols], raw[:, k, cols], g32[:, k, cols], start=(k == 0), stop=(k == KC - 1))
            mm.then_inc(c_mm, 1)

            def transposes(n):
                for k in range(KC):
                    for i in range(NT):
                        pe.wait_ge(s_norm, NT * (0, 2, 3)[n] + i + 1)
                        mm = pe.transpose(bank[k][:, i * P:(i + 1) * P], xn[:, i, k * P:(k + 1) * P], ident[:, :])
                    mm.then_inc(xT_mm, 1)

            def project(slot, banks, done, width=P, slot_hi=None):
                for c in range(KC):
                    for k in range(KC):
                        cols = slice(c * P, (c + 1) * P)
                        mm = three(pe, bank[banks + c][:, :], hi[:, 4 * slot + k, cols], lo[:, 4 * slot + k, cols],
                                   gh[:, k, :], gl[:, k, :], k == 0, k == KC - 1)
                    mm.then_inc(done, 1)

            pe.wait_ge(consts, 12 + NE)
            transposes(0)
            pe.wait_ge(xT_lo, KC)
            pe.wait_ge(w_lo, 1)
            pe.wait_ge(c_done, 1)
            project(1, 4, q_mm)

            def gram(b, first):
                for c in range(CH + 1):
                    r, kk = chunk(c)
                    pe.wait_ge(ctx_lo, b * 4 + c + 1)
                    if c == 0 and not first:
                        pe.wait_ge(g_act, b * 2)
                        pe.wait_ge(g_dve, b)
                    for t in range(r.start, r.stop):
                        start, stop = t == 0, t == NSLOT - 1
                        for m in range(KC):
                            n0 = gram_cols(m)
                            dst = bank[m][:, n0:D] if m < 2 else bank[2][:, (m - 2) * 2 * P:(m - 1) * 2 * P]
                            rows = slice(m * P, (m + 1) * P)
                            wh, wl = hi[0:kk, t, rows], lo[0:kk, t, rows]
                            xh, xl = hi[0:kk, t, n0:D], lo[0:kk, t, n0:D]
                            pe.matmul(dst, wh, xh, start=start and m < 3, stop=False, skip_group_check=m > 1)
                            pe.matmul(dst, wh, xl, start=False, stop=False, skip_group_check=m > 1)
                            mm = pe.matmul(dst, wl, xh, start=False, stop=stop, skip_group_check=m > 1)
                    mm.then_inc(gram_mm, 1)

            def g_transposes(b, first):
                pe.wait_ge(g_act, b * 2 + 2)
                pe.wait_ge(g_dve, b + 1)
                if first:
                    pe.wait_ge(q_done, KC)
                else:
                    pe.wait_ge(gl_done, b * 5)
                for n in range(1, KC):
                    pe.transpose(bank[3][:, (n - 1) * P:n * P], g32[:, 0, n * P:(n + 1) * P], ident[:, :])
                for n in range(2, KC):
                    mm = pe.transpose(bank[4][:, (n - 2) * P:(n - 1) * P], g32[:, 1, n * P:(n + 1) * P], ident[:, :])
                mm.then_inc(gt_mm, 1)

            def kv_of(b, first):
                pe.wait_ge(gl_done, b * 5 + 5)
                if first:
                    pe.wait_ge(w_lo, 2)
                    pe.wait_ge(q_done, KC)
                    pe.wait_ge(ld_wk, 16)
                for m in range(KC):
                    if not (first and m < 2):
                        pe.wait_ge(m_done, b * 4 + m - 1)
                    for k in range(KC):
                        rows = slice(m * P, (m + 1) * P)
                        mm = three(pe, bank[5 + m % 2][:, :], gh[:, k, rows], gl[:, k, rows], wvh[:, k, :], wvl[:, k, :],
                                   k == 0, k == KC - 1)
                    mm.then_inc(m_mm, 1)
                pe.wait_ge(m_done, b * 4 + 4)
                if not first:
                    pe.wait_ge(kv_done, b)
                for c in range(KC):
                    for k in range(KC):
                        cols = slice(c * P, (c + 1) * P)
                        mm = pe.matmul(bank[7][:, cols], wk[:, k, cols], mb[:, k, cols], start=(k == 0), stop=(k == KC - 1))
                mm.then_inc(kv_mm, 1)

            gram(0, True)
            g_transposes(0, True)
            gram(1, False)
            kv_of(0, True)
            g_transposes(1, False)
            with pe.Fori(2, B) as b:
                gram(b, False)
                kv_of(b - 1, False)
                g_transposes(b, False)
            kv_of(B - 1, False)

            pe.wait_ge(sum_out, B)
            for b in range(B):
                for k in range(KC):
                    mm = pe.matmul(bank[0][:, k * B + b:k * B + b + 1], sx[:, b, k * P:(k + 1) * P], ones[:, :], start=True, stop=True)
            mm.then_inc(s_mm, 1)
            pe.wait_ge(s_done, 1)
            for n, w in ((1, wk), (2, g32)):
                if n == 2:
                    pe.wait_ge(ld_wv2, 16)
                for k in range(KC):
                    mm = pe.matmul(bank[n][0:B, :], scol[:, k, :], w[:, k, :], start=(k == 0), stop=(k == KC - 1))
                mm.then_inc(r_mm, 1)

            def rank2(b):
                if b == 0:
                    pe.wait_ge(ld_rows, 48)
                    pe.wait_ge(ld_bvrow, 16)
                if b >= 2:
                    pe.wait_ge(r2_tmp, b - 1)
                for c in range(KC):
                    cols = slice(c * P, (c + 1) * P)
                    mm = pe.matmul(bank[3 + b % 2][:, cols], a2[:, b, cols], b2[:, b, cols], start=True, stop=True)
                mm.then_inc(r2_mm, 1)

            def attend(i):
                if i == 2:
                    pe.wait_ge(kv_done, B)
                for b in (2 * i, 2 * i + 1):
                    pe.wait_ge(r2_done, b + 1)
                    for c in range(KC):
                        cols = slice(c * P, (c + 1) * P)
                        p0 = S * (b % 2)
                        mm = pe.matmul(bank[(5, 6, 7, 0)[i]][p0:p0 + S, cols], qT[:, c, b * S:(b + 1) * S], kv[:, b, cols],
                                       start=True, stop=True)
                mm.then_inc(att_mm, 1)

            for b in range(B):
                rank2(b)
                if b >= 3 and b % 2:
                    attend((b - 3) // 2)
            attend(NT - 1)

            transposes(1)
            pe.wait_ge(w_lo, 3)
            pe.wait_ge(xT_lo, 2 * KC)
            project(0, 4, q_mm)
            for g in range(NG):
                for c in range(KC):
                    pe.wait_ge(q_done, KC + c + 1)
                    mm = pe.matmul(bank[g][:, c * P:(c + 1) * P], qT[:, c, g * P:(g + 1) * P], cb[:, c, :], start=True, stop=True)
                mm.then_inc(vv_mm, 1)

            def logits_1(u):
                c, j = u // 4, slice(D1 * (u % 4), D1 * (u % 4) + D1)
                s = bank[u % 2]
                if u == 0:
                    pe.wait_ge(bfconst, 2 * (P // 16) + 2)
                    pe.wait_ge(vv_done, NG)
                if u < 2 or u % 4 == 0:
                    pe.wait_ge(qq_lo, c + 1)
                if u >= 2:
                    pe.wait_ge(e_done, 4 * (u - 1))
                pe.matmul(s[:, :], identb[:, :], posmask[:, :], start=True, stop=False)
                pe.matmul(s[:, :], neghalf[j, :], wvh[j, c, :], start=False, stop=False)
                pe.matmul(s[:, :], neghalf[j, :], wvl[j, c, :], start=False, stop=False)
                for g in range(NG):
                    q = qT[j, c, g * P:(g + 1) * P]
                    mm = pe.matmul(s[:, g * P:(g + 1) * P], q, q, start=False, stop=(g == NG - 1))
                mm.then_inc(lg_mm, 1)

            def transpose_e(u):
                pe.wait_ge(e_done, 4 * (u + 1))
                if u >= 2:
                    pe.wait_ge(eT_done, u - 1)
                for s in range(4):
                    mm = pe.transpose(bank[2 + u % 2][:, s * P:(s + 1) * P], ering[:, u % 2, s * P:(s + 1) * P], ident[:, :])
                mm.then_inc(eT_mm, 1)

            def weigh(u, eT, values, d):
                pe.wait_ge(eT_done, min(u, H1 + 7) + 1)
                if u >= 2:
                    pe.wait_ge(pv_done, u - 1)
                for s in range(4):
                    mm = pe.matmul(bank[4 + u % 2][:, s * (d + 1):(s + 1) * (d + 1)], eT[:, s * P:(s + 1) * P], values(s),
                                   start=True, stop=True)
                mm.then_inc(pv_mm, 1)

            for u in range(H1 + 2):
                if u < H1:
                    logits_1(u)
                if 1 <= u <= H1:
                    transpose_e(u - 1)
                if u >= 2:
                    h = u - 2
                    if h == 0:
                        pe.wait_ge(vv_one, 1)
                    weigh(h, kv[:, h % 2, :], lambda s: vv[:, s, h, :], D1)
            pe.wait_ge(pv_done, H1)
            for k in range(KC):
                for g in range(NG):
                    mm = pe.transpose(bank[k][:, g * P:(g + 1) * P], mb[:, g, k * P:(k + 1) * P], ident[:, :])
                mm.then_inc(pT_mm, 1)
            for i in range(NT):
                for k in range(KC):
                    if i == 0:
                        pe.wait_ge(pT_lo, k + 1)
                        pe.wait_ge(w_lo, 4)
                    rows = slice(i * P, (i + 1) * P)
                    mm = three(pe, bank[4 + i][:, :], wvh[:, k, rows], wvl[:, k, rows], hi[:, 4 + k, :], lo[:, 4 + k, :],
                               k == 0, k == KC - 1)
                mm.then_inc(op_mm, 1)

            pe.wait_ge(pT_lo, KC)
            transposes(2)
            pe.wait_ge(xT_lo, 3 * KC)
            pe.wait_ge(w_lo, 5)
            project(0, 4, q_mm)
            pe.wait_ge(w_lo, 6)
            project(1, 0, q_mm)
            pe.wait_ge(wg_lo_done, 1)
            pe.wait_ge(q_done, 2 * KC + 4)
            for k in range(KC):
                mm = three(pe, bank[4][:, :], wg_hi[:, k, :], wg_lo[:, k, :], gh[:, k, :], gl[:, k, :], k == 0, k == KC - 1)
            mm.then_inc(gl_mm, 1)
            pe.wait_ge(gT_done, 1)
            ne = H2 * NE
            for i in range(NT):
                mm = pe.transpose(bank[5][:, i * ne:(i + 1) * ne], gateT[0:ne, i * P:(i + 1) * P], ident[0:ne, 0:ne])
            mm.then_inc(gl2_mm, 1)

            def logits_2(u):
                i, hh = (u - H1) // 2, (u - H1) % 2
                s = bank[u % 2]
                if u == H1:
                    pe.wait_ge(k_done, KC)
                if u >= H1 + 2:
                    pe.wait_ge(e_done, 4 * (u - 1))
                pe.matmul(s[:, :], identb[:, :], causal[:, :], start=True, stop=False)
                for n in range(4):
                    h = 2 * n + hh
                    j, c, rows = slice(D2 * (h % 2), D2 * (h % 2) + D2), h // 2, slice(i * P, (i + 1) * P)
                    mm = pe.matmul(s[:, n * P:(n + 1) * P], qT[j, c, rows], mb[j, c, rows], start=False, stop=(n == 3))
                mm.then_inc(lg_mm, 1)

            for u in range(H1, H1 + 9):
                if u < H1 + 8:
                    logits_2(u)
                if u > H1:
                    transpose_e(u - 1)

            def value_products(e, slot, first):
                pe.wait_ge(w_lo, e + 7)
                for i in range(NT):
                    if first:
                        pe.wait_ge(ge_done, 1)
                    else:
                        pe.wait_ge(v_gated, e * NT + i - 3)
                    for k in range(KC):
                        rows = slice(i * P, (i + 1) * P)
                        mm = three(pe, bank[4 + i][:, :], gh[:, k, rows], gl[:, k, rows], hi[:, 4 * slot + k, :],
                                   lo[:, 4 * slot + k, :], k == 0, k == KC - 1)
                    mm.then_inc(v_mm, 1)

            value_products(0, 0, True)
            with pe.Fori(0, NE // 2 - 1) as j:
                e = j * 2 + 1
                value_products(e, 1, False)
                value_products(e + 1, 0, False)
            value_products(NE - 1, 1, False)
            pe.wait_ge(v_added, NE * NT)
            pe.wait_ge(v_zero, 2)
            for u in range(H1, H1 + 8):
                i, hh = (u - H1) // 2, (u - H1) % 2
                weigh(u, kv[:, u - H1, :], lambda s: vals[:, i, 2 * s + hh, :], D2)

            def gated_T(e):
                pe.wait_ge(og_done, e * NT + NT)
                for k in range(KC):
                    if not isinstance(e, int) or e:
                        pe.wait_ge(oT_lo, e * 4 + k - 3)
                    for i in range(NT):
                        mm = pe.transpose(bank[4 + k][:, i * P:(i + 1) * P], xn[:, i, k * P:(k + 1) * P], ident[:, :])
                    mm.then_inc(oT_mm, 1)

            def output_products(e, slot, bh, bl, first, last):
                pe.wait_ge(oT_lo, e * 4 + 4)
                pe.wait_ge(w_lo, e + (7 + NE))
                for i in range(NT):
                    for k in range(KC):
                        rows = slice(i * P, (i + 1) * P)
                        mm = three(pe, bank[i][:, :], bh[:, k, rows], bl[:, k, rows], hi[:, 4 * slot + k, :],
                                   lo[:, 4 * slot + k, :], first and k == 0, last and k == KC - 1)
                    if last:
                        mm.then_inc(out_mm, 1)
                if not last:
                    mm.then_inc(out_mm, 1)

            gated_T(0)
            gated_T(1)
            output_products(0, 0, wvh, wvl, True, False)
            with pe.Fori(0, NE // 2 - 1) as j:
                e = j * 2 + 1
                gated_T(e + 1)
                output_products(e, 1, gh, gl, False, False)
                gated_T(e + 2)
                output_products(e + 1, 0, wvh, wvl, False, False)
            output_products(NE - 1, 1, gh, gl, False, True)

        @block.vector
        def _(dve):
            def layer_norm(n):
                src = xn if n == 1 else xres
                for i in range(NT):
                    if n == 1:
                        dve.wait_ge(y_done, i + 1)
                    dve.bn_stats(stats[:, i, :], src[:, i, :]).then_inc(s_stats, 1)
                for i in range(NT):
                    dve.wait_ge(s_stats, NT * n + i + 1)
                    dve.bn_aggr(mv[:, i, :], stats[:, i, :]).then_inc(s_aggr, 1)
                dve.wait_ge(s_aggr, NT * n + NT)
                dve.tensor_scalar(vareps[:, :], mv[:, :, 1], LN_EPS, None, ALU.add).then_inc(s_var, 1)
                dve.wait_ge(s_rstd, n + 1)
                for i in range(NT):
                    dve.tensor_scalar(xn[:, i, :], src[:, i, :], mv[:, i, 0:1], rstd[:, i:i + 1],
                                      ALU.subtract, ALU.mult).then_inc(s_norm, 1)

            def xT_low(n):
                for k in range(KC):
                    dve.wait_ge(xT_hi, KC * n + k + 1)
                    dve.tensor_tensor(gl[:, k, :], bank[k][:, :], gh[:, k, :].bitcast(F32), ALU.subtract).then_inc(xT_lo, 1)

            dve.wait_ge(ld_x, 16)
            layer_norm(0)
            dve.wait_ge(w_hi, 1)
            dve.tensor_tensor(lo[:, half(1), :], raw[:, half(1), :], hi[:, half(1), :].bitcast(F32), ALU.subtract).then_inc(w_lo, 1)
            dve.wait_ge(c_mm, 1)
            dve.wait_ge(consts, 12 + NE)
            dve.scalar_tensor_tensor(out=cb[:, :, :], in0=bank[7][:, :].rearrange("p (k n) -> p k n", n=P), scalar=INV1,
                                     in1=headmask[:, :].unsqueeze(1).broadcast_to([P, KC, P]),
                                     op0=ALU.mult, op1=ALU.mult).then_inc(c_done, 1)
            xT_low(0)
            dve.wait_ge(w_hi, 2)
            dve.tensor_tensor(wvl[:, :, :], raw[:, half(2), :], wvh[:, :, :].bitcast(F32), ALU.subtract).then_inc(w_lo, 1)
            dve.wait_ge(ld_par, 80)
            for k in range(KC):
                dve.wait_ge(q_mm, k + 1)
                dve.tensor_scalar(qT[:, k, :], bank[4 + k][:, :], bq[:, k:k + 1], INV1, ALU.add, ALU.mult).then_inc(q_done, 1)

            def ctx_low(b, c):
                r, k = chunk(c)
                dve.wait_ge(ctx_hi, b * 4 + c + 1)
                dve.tensor_tensor(lo[0:k, r, :], raw[0:k, r, :], hi[0:k, r, :].bitcast(F32), ALU.subtract).then_inc(ctx_lo, 1)

            def g_copy(b, first):
                dve.wait_ge(gram_mm, b * 4 + 4)
                if not first:
                    dve.wait_ge(gh_done, b * 5)
                    dve.wait_ge(gt_mm, b)
                dve.tensor_copy(g32[:, 2:4, 2 * P:D], bank[2][:, :].rearrange("p (m n) -> p m n", m=2)).then_inc(g_dve, 1)

            def gl_low(b):
                def sub(o, i0, i1):
                    dve.tensor_tensor(o, i0, i1.bitcast(F32), ALU.subtract).then_inc(gl_done, 1)
                dve.wait_ge(gh_done, b * 5 + 3)
                dve.wait_ge(g_dve, b + 1)
                sub(gl[:, 0, :], g32[:, 0, :], gh[:, 0, :])
                sub(gl[:, 1, P:D], g32[:, 1, P:D], gh[:, 1, P:D])
                sub(gl[:, 2:4, 2 * P:D], g32[:, 2:4, 2 * P:D], gh[:, 2:4, 2 * P:D])
                dve.wait_ge(gh_done, b * 5 + 5)
                sub(gl[:, 1:4, 0:P], bank[3][:, 0:3 * P].rearrange("p (m n) -> p m n", n=P), gh[:, 1:4, 0:P])
                sub(gl[:, 2:4, P:2 * P], bank[4][:, 0:2 * P].rearrange("p (m n) -> p m n", n=P), gh[:, 2:4, P:2 * P])

            def kv_copy(b):
                dve.wait_ge(kv_mm, b + 1)
                dve.tensor_tensor(kv[:, b, :].rearrange("p (k n) -> p k n", n=P), bank[7][:, :].rearrange("p (k n) -> p k n", n=P),
                                  headmask[:, :].unsqueeze(1).broadcast_to([P, KC, P]), ALU.mult).then_inc(kv_done, 1)

            def sum_copy(b):
                dve.wait_ge(ctx_sum, b * NADD + NADD)
                dve.tensor_scalar(sx[:, b, :], psum_tmp[:, :], 1.0, None, ALU.mult).then_inc(sum_out, 1)

            for c in range(4):
                ctx_low(0, c)
            g_copy(0, True)
            sum_copy(0)
            ctx_low(1, 0)
            gl_low(0)
            with dve.Fori(1, B - 1) as b:
                for c in range(1, 4):
                    ctx_low(b, c)
                g_copy(b, False)
                sum_copy(b)
                ctx_low(b + 1, 0)
                kv_copy(b - 1)
                gl_low(b)
            for c in range(1, 4):
                ctx_low(B - 1, c)
            g_copy(B - 1, False)
            sum_copy(B - 1)
            kv_copy(B - 2)
            gl_low(B - 1)
            kv_copy(B - 1)

            dve.wait_ge(r_mm, 2)
            dve.scalar_tensor_tensor(out=rv, in0=bv8[:, :], scalar=float(T), in1=bank[2][0:B, :],
                                     op0=ALU.mult, op1=ALU.add).then_inc(rv_done, 1)
            for b in range(B):
                dve.wait_ge(r2_mm, b + 1)
                t = mb[:, b % 2, :]
                dve.tensor_tensor(t.rearrange("p (k n) -> p k n", n=P), bank[3 + b % 2][:, :].rearrange("p (k n) -> p k n", n=P),
                                  headmask[:, :].unsqueeze(1).broadcast_to([P, KC, P]), ALU.mult).then_inc(r2_tmp, 1)
                dve.wait_ge(r2_tmp, b + 1)
                dve.wait_ge(kv_done, b + 1)
                dve.tensor_tensor(kv[:, b, :], kv[:, b, :], t, ALU.add).then_inc(r2_done, 1)
            dve.wait_ge(s_norm, NT)
            for i in range(NT):
                dve.wait_ge(att_mm, i + 1)
                dve.tensor_tensor(xn[:, i, :], xn[:, i, :], bank[(5, 6, 7, 0)[i]][:, :], ALU.add).then_inc(y_done, 1)
            layer_norm(1)
            for i in range(NT):
                dve.wait_ge(s_norm, NT + i + 1)
                dve.tensor_tensor(mb[:, i, :], xn[:, i, :], gamma[:, :], ALU.mult).then_inc(z_done, 1)
            for i in range(NT):
                dve.wait_ge(z_done, i + 1)
                dve.wait_ge(xb_done, i + 1)
                dve.tensor_tensor(xres[:, i, :], xres[:, i, :], mb[:, i, :], ALU.add).then_inc(x1_done, 1)
            dve.wait_ge(x1_done, NT)
            layer_norm(2)

            def w_low(n, slot):
                dve.wait_ge(w_hi, n + 3)
                dve.tensor_tensor(lo[:, half(slot), :], raw[:, half(slot), :], hi[:, half(slot), :].bitcast(F32),
                                  ALU.subtract).then_inc(w_lo, 1)

            w_low(W_Q1, 0)
            w_low(W_OUT, 1)
            xT_low(1)
            for k in range(KC):
                dve.wait_ge(qq_hi, k + 1)
                dve.tensor_tensor(wvl[:, k, :], xn[:, k, :], wvh[:, k, :].bitcast(F32), ALU.subtract).then_inc(qq_lo, 1)

            def unit_max(u, scale):
                dve.wait_ge(lg_mm, u + 1)
                if u >= 2:
                    dve.wait_ge(e_done, 4 * (u - 1))
                blocks4 = bank[u % 2][:, :].rearrange("p (s n) -> p s n", n=P)
                dve.tensor_reduce(rz[:, u % 2, :], blocks4, AX_X, ALU.max).then_inc(mx_done, 1)
                dve.wait_ge(mx_done, u + 1)
                dve.tensor_scalar(negmax[:, u % 2, :], rz[:, u % 2, :], -scale, None, ALU.mult).then_inc(nm_done, 1)

            def unit_eT(u, dst):
                dve.wait_ge(eT_mm, u + 1)
                dve.tensor_copy(dst, bank[2 + u % 2][:, :]).then_inc(eT_done, 1)

            def unit_out(u, dst, d):
                dve.wait_ge(pv_mm, u + 1)
                o = bank[4 + u % 2][:, 0:4 * (d + 1)].rearrange("p (s e) -> p s e", e=d + 1)
                rzu = stats[:, :, u % 2]
                if u >= 2:
                    dve.wait_ge(pv_done, u - 1)
                dve.reciprocal(rzu, o[:, :, d]).then_inc(rz_done, 1)
                dve.wait_ge(rz_done, u + 1)
                dve.tensor_tensor(dst, o[:, :, 0:d], rzu.unsqueeze(2).broadcast_to([P, 4, d]), ALU.mult).then_inc(pv_done, 1)

            for u in range(H1 + 2):
                if u < H1:
                    unit_max(u, 2.0 * INV1)
                if 1 <= u <= H1:
                    if u >= 3:
                        dve.wait_ge(pv_mm, u - 2)
                    unit_eT(u - 1, kv[:, (u - 1) % 2, :])
                if u >= 2:
                    h = u - 2
                    unit_out(h, mb[:, :, h * D1:(h + 1) * D1], D1)
            w_low(W_Q2, 0)
            for k in range(KC):
                dve.wait_ge(pT_hi, k + 1)
                dve.tensor_tensor(wvl[:, k, :].rearrange("p (t g q) -> p g t q", g=NG, q=16),
                                  bank[k][:, :].rearrange("p (g t q) -> p g t q", g=NG, q=16),
                                  wvh[:, k, :].bitcast(F32).rearrange("p (t g q) -> p g t q", g=NG, q=16),
                                  ALU.subtract).then_inc(pT_lo, 1)
            for i in range(NT):
                dve.wait_ge(op_mm, i + 1)
                dve.wait_ge(ob_done, i + 1)
                dve.tensor_tensor(xres[:, i, :], xres[:, i, :], bank[4 + i][:, :], ALU.add).then_inc(x2_done, 1)
            dve.wait_ge(x2_done, NT)
            layer_norm(3)
            w_low(W_K2, 1)
            dve.wait_ge(wg_hi_done, 2)
            dve.tensor_tensor(wg_lo, wg_raw, wg_hi.bitcast(F32), ALU.subtract).then_inc(wg_lo_done, 1)
            xT_low(2)
            for k in range(KC):
                dve.wait_ge(q_mm, 3 * KC + k + 1)
                dve.tensor_copy(mb[:, k, :], bank[k][:, :]).then_inc(k_done, 1)

            step = [0]

            def link(ins):
                step[0] += 1
                ins.then_inc(g_step, 1)
                dve.wait_ge(g_step, step[0])

            def by_head(t):
                return t.rearrange("p (g e) -> p g e", e=NE)

            dve.wait_ge(ge_done, 1)
            link(dve.tensor_scalar(gates, gates, 1.0, None, ALU.add))
            link(dve.reciprocal(gates, gates))
            link(dve.tensor_reduce(gmax[:, :], by_head(gates), AX_X, ALU.max))
            link(dve.tensor_tensor(by_head(gsel), by_head(gates), gmax[:, :].unsqueeze(2).broadcast_to([P, NT * H2, NE]), ALU.is_equal))
            link(dve.tensor_tensor(gsel, gsel, tie[:, :], ALU.mult))
            link(dve.tensor_reduce(gmax[:, :], by_head(gsel), AX_X, ALU.max))
            link(dve.tensor_tensor(by_head(gsel), by_head(gsel), gmax[:, :].unsqueeze(2).broadcast_to([P, NT * H2, NE]), ALU.is_equal))
            dve.tensor_tensor(gm, gsel, gates, ALU.mult).then_inc(gm_done, 1)

            w_low(W_VE, 0)
            for u in range(H1, H1 + 9):
                if u < H1 + 8:
                    unit_max(u, 1.0)
                if u > H1:
                    if u == H1 + 1:
                        dve.wait_ge(pv_mm, H1)
                    unit_eT(u - 1, kv[:, u - 1 - H1, :])
            w_low(W_VE + 1, 1)

            def gated(e, first):
                g3 = gm.rearrange("p (i h e) -> p i h e", i=NT, h=H2)
                for i in range(NT):
                    dve.wait_ge(v_mm, e * NT + i + 1)
                    if not (first and i < 2):
                        dve.wait_ge(v_added, e * NT + i - 1)
                    g = g3[:, i, :, bass.ds(e, 1)] if not isinstance(e, int) else g3[:, i, :, e:e + 1]
                    dve.tensor_tensor(tmp[:, i % 2, :].rearrange("p (h k) -> p h k", k=D2),
                                      bank[4 + i][:, :].rearrange("p (h k) -> p h k", k=D2),
                                      g.broadcast_to([P, H2, D2]), ALU.mult).then_inc(v_gated, 1)

            def expert_lo(slot, count):
                dve.wait_ge(w_hi, count)
                dve.tensor_tensor(lo[:, half(slot), :], raw[:, half(slot), :], hi[:, half(slot), :].bitcast(F32),
                                  ALU.subtract).then_inc(w_lo, 1)

            dve.wait_ge(gm_done, 1)
            gated(0, True)
            expert_lo(0, 9)
            with dve.Fori(0, NE // 2 - 1) as j:
                e = j * 2 + 1
                gated(e, False)
                expert_lo(1, e + 9)
                gated(e + 1, False)
                expert_lo(0, e + 10)
            gated(NE - 1, False)
            expert_lo(1, NE + 8)

            for u in range(H1, H1 + 8):
                i, hh = (u - H1) // 2, (u - H1) % 2
                unit_out(u, mb[:, i, :].rearrange("p (s hh e) -> p s hh e", hh=2, e=D2)[:, :, hh, :], D2)

            def oT_low(e, bufh, bufl):
                for k in range(KC):
                    dve.wait_ge(oT_hi, e * 4 + k + 1)
                    dve.tensor_tensor(bufl[:, k, :], bank[4 + k][:, :], bufh[:, k, :].bitcast(F32), ALU.subtract).then_inc(oT_lo, 1)

            def gate_out(e):
                g3 = gm.rearrange("p (i h e) -> p i h e", i=NT, h=H2)
                for i in range(NT):
                    g = g3[:, i, :, bass.ds(e, 1)] if not isinstance(e, int) else g3[:, i, :, e:e + 1]
                    if i == 0:
                        if isinstance(e, int) and e == 0:
                            dve.wait_ge(pv_done, H1 + 8)
                        else:
                            dve.wait_ge(oT_mm, e * 4)
                    dve.tensor_tensor(xn[:, i, :].rearrange("p (h k) -> p h k", k=D2),
                                      mb[:, i, :].rearrange("p (h k) -> p h k", k=D2),
                                      g.broadcast_to([P, H2, D2]), ALU.mult).then_inc(og_done, 1)

            gate_out(0)
            gate_out(1)
            oT_low(0, wvh, wvl)
            oT_low(1, gh, gl)
            with dve.Fori(0, NE // 2 - 1) as j:
                e = j * 2 + 1
                for s, bh, bl in ((0, wvh, wvl), (1, gh, gl)):
                    gate_out(e + (s + 1))
                    expert_lo(s, e + (16 + s))
                    oT_low(e + (s + 1), bh, bl)
            for i in range(NT):
                dve.wait_ge(out_mm, NE + i)
                dve.tensor_tensor(xres[:, i, :], xres[:, i, :], bank[i][:, :], ALU.add).then_inc(fin, 1)


def kernel(x, ctx_1024, L0_xattn_Wq, L0_xattn_bq, L0_xattn_Wk, L0_xattn_bk, L0_xattn_Wv, L0_xattn_bv,
           L0_xattn_ln_gamma, L0_xattn_ln_beta, L0_attn_q_weight, L0_attn_v_weight, L0_attn_out_w, L0_attn_out_b,
           L0_ffn_w_q, L0_ffn_w_k, L0_ffn_w_gate, L0_ffn_value_experts, L0_ffn_output_experts):
    import numpy as np
    import concourse.bacc as bacc
    from concourse.bass_utils import run_bass_kernel_spmd

    D = x.shape[-1]
    E = L0_ffn_value_experts.shape[0]
    host = {
        "x": x, "ctx_1024": ctx_1024,
        "WqT": L0_xattn_Wq.T, "WkT": L0_xattn_Wk.T, "WvT": L0_xattn_Wv.T,
        "bq": L0_xattn_bq, "bk": L0_xattn_bk, "bv": L0_xattn_bv,
        "gamma": L0_xattn_ln_gamma, "beta": L0_xattn_ln_beta,
        "qw": L0_attn_q_weight.reshape(D, D), "vw": L0_attn_v_weight.reshape(D, D),
        "owT": L0_attn_out_w.T, "out_b": L0_attn_out_b,
        "wq2": L0_ffn_w_q, "wk2": L0_ffn_w_k, "wg": L0_ffn_w_gate,
        "ve": L0_ffn_value_experts.transpose(0, 2, 1, 3).reshape(E, D, D),
        "oe": L0_ffn_output_experts.reshape(E, D, D),
    }
    nc = bacc.Bacc("TRN2", target_bir_lowering=False, num_devices=1)
    arrays, drams = {}, {}
    for name, v in host.items():
        v = np.ascontiguousarray(v)
        arrays[f"in_{name}"] = v
        drams[name] = nc.dram_tensor(f"in_{name}", v.shape, mybir.dt.from_np(v.dtype), kind="ExternalInput").ap()
    out = nc.dram_tensor("out", x.shape, F32, kind="ExternalOutput").ap()
    perceiver_block(nc, drams, out)
    r = run_bass_kernel_spmd(nc, [arrays], core_ids=[0])
    return r.results[0]["out"]
```

```python
from contextlib import ExitStack
from math import sqrt

import concourse.bass as bass
from concourse import mybir

F32 = mybir.dt.float32
F32R = mybir.dt.float32r
BF16 = mybir.dt.bfloat16
ALU = mybir.AluOpType
ACT = mybir.ActivationFunctionType
AX_X = mybir.AxisListType.X

P = 128
MASKED = -1e30
LN_EPS = 1e-5


def perceiver_block(nc, a, out):
    B, S, D = a["x"].shape
    T = a["ctx_1024"].shape[1]
    N = B * S
    KC = D // P
    NT = N // P
    ROWS = 4
    CH = T // (P * ROWS)
    REM = T - CH * P * ROWS
    NSLOT = CH * ROWS + 1
    H1 = 16
    D1 = D // H1
    H2 = 8
    D2 = D // H2
    NE = 8
    NG = S // 16
    INV1 = 1.0 / sqrt(D1)
    SCALE2 = float(D2) ** -0.5
    NADD = NSLOT - 1
    SUMMED = [ROWS * c + ROWS - 1 for c in range(CH)] + [NADD]
    assert (N, D, KC, NT, CH, NG) == (512, 512, 4, 4, 3, 4) and 0 < REM < P

    with ExitStack() as ctx:
        def sb(name, shape, dt=F32):
            return ctx.enter_context(nc.sbuf_tensor(name, shape, dt))

        def sem(name):
            return ctx.enter_context(nc.semaphore(name))

        raw = sb("raw", [P, NSLOT, D])
        hi = sb("hi", [P, NSLOT, D], F32R)
        lo = sb("lo", [P, NSLOT, D], F32R)
        xres = sb("xres", [P, NT, D])
        xn = sb("xn", [P, NT, D])
        qT = sb("qT", [P, KC, N])
        g32 = sb("g32", [P, KC, D])
        mb = sb("mb", [P, KC, D])
        wk = sb("wk", [P, KC, D])
        kv = sb("kv", [P, B, D])
        sx = sb("sx", [P, B, D])
        wvh = sb("wvh", [P, KC, D], F32R)
        wvl = sb("wvl", [P, KC, D], F32R)
        gh = sb("gh", [P, KC, D], F32R)
        gl = sb("gl", [P, KC, D], F32R)
        gamma = sb("gamma", [P, D])
        beta = sb("beta", [P, D])
        out_b = sb("out_b", [P, D])
        bv8 = sb("bv8", [B, D])
        psum_tmp = sb("psum_tmp", [P, D])
        bq = sb("bq", [P, KC])
        ident = sb("ident", [P, P])
        identb = sb("identb", [P, P], BF16)
        headmask = sb("headmask", [P, P])
        posmask = sb("posmask", [P, 4 * P], BF16)
        causal = sb("causal", [P, 4 * P], BF16)
        neghalf = sb("neghalf", [P, P], F32R)
        cb = sb("cb", [P, KC, P])
        scol = sb("scol", [P, KC, B])
        ones = sb("ones", [P, 1])
        expo = sb("expo", [P, NT])
        stats = sb("stats", [P, NT, 6])
        mv = sb("mv", [P, NT, 2])
        vareps = sb("vareps", [P, NT])
        rstd = sb("rstd", [P, NT])
        negmax = sb("negmax", [P, 2, 4])
        rz = sb("rz", [P, 2, 4])

        a2 = sx[0:2, :, :]
        b2 = raw[0:2, 4:12, :]
        wv_raw = sx[:, 4:8, :]
        rk = raw[0:B, 12, :]
        rv = psum_tmp[0:B, :]
        tmp = raw[:, 9:11, :]
        wg_raw = raw[:, 8, :].rearrange("p (k n) -> p k n", n=P)
        wg_hi = hi[:, 8, :].rearrange("p (k n) -> p k n", n=P)
        wg_lo = lo[:, 8, :].rearrange("p (k n) -> p k n", n=P)
        sxf = sx[:, :, :].rearrange("p b d -> p (b d)")
        vv = sxf[:, 0:NG * H1 * (D1 + 1)].rearrange("p (g h e) -> p g h e", g=NG, h=H1)
        vals = sxf[:, 0:NT * H2 * (D2 + 1)].rearrange("p (i h e) -> p i h e", i=NT, h=H2)
        ering = sxf[:, 2112:2112 + 2 * D].rearrange("p (r n) -> p r n", r=2)
        gateT = sxf[:, 3136:3136 + N]
        gsc = raw[:, 11, :].rearrange("p (r n) -> p r n", r=2)
        gates = gsc[:, 0, :]
        gsel = gsc[:, 1, :]
        gm = sxf[:, 3648:3648 + NT * H2 * NE]
        tie = sb("tie", [P, NT * H2 * NE])
        gmax = sb("gmax", [P, NT * H2])

        bank = [ctx.enter_context(nc.psum_tensor(f"bank{n}", [P, 512], F32)) for n in range(8)]

        ld_x, ld_qv, ld_wq, ld_wv, ld_wk, ld_par = (sem(s) for s in ("ld_x", "ld_qv", "ld_wq", "ld_wv", "ld_wk", "ld_par"))
        ld_ctx = [sem(f"ld_ctx{c}") for c in range(CH + 1)]
        ld_wv2, ld_rows, ld_bvrow, ld_wg = (sem(s) for s in ("ld_wv2", "ld_rows", "ld_bvrow", "ld_wg"))
        ld_w = [sem("ld_w0"), sem("ld_w1")]
        consts, bfconst = sem("consts"), sem("bfconst")
        c_mm, c_done, ld_bq = sem("c_mm"), sem("c_done"), sem("ld_bq")
        s_stats, s_aggr, s_var, s_rstd, s_norm = (
            [sem(f"{s}{n}") for n in range(4)] for s in ("s_stats", "s_aggr", "s_var", "s_rstd", "s_norm"))
        xT_mm, xT_hi, xT_lo = sem("xT_mm"), sem("xT_hi"), sem("xT_lo")
        w_hi, w_lo = sem("w_hi"), sem("w_lo")
        q_mm, q_done = sem("q_mm"), sem("q_done")
        ctx_hi, ctx_lo, ctx_sum, sum_out = (sem(s) for s in ("ctx_hi", "ctx_lo", "ctx_sum", "sum_out"))
        gram_mm, g_act, g_dve, gt_mm, gh_done, gl_done = (sem(s) for s in ("gram_mm", "g_act", "g_dve", "gt_mm", "gh_done", "gl_done"))
        m_mm, m_done, kv_mm, kv_done = (sem(s) for s in ("m_mm", "m_done", "kv_mm", "kv_done"))
        s_mm, s_done, r_mm, rk_done, rv_done, r2_mm, r2_tmp, r2_even, r2_done = (
            sem(s) for s in ("s_mm", "s_done", "r_mm", "rk_done", "rv_done", "r2_mm", "r2_tmp", "r2_even", "r2_done"))
        att_mm, y_done, xb_done, z_done, x1_done, ob_done = (
            sem(s) for s in ("att_mm", "y_done", "xb_done", "z_done", "x1_done", "ob_done"))
        qq_done, qq_hi, qq_lo, vv_mm, vv_done, vv_one = (sem(s) for s in ("qq_done", "qq_hi", "qq_lo", "vv_mm", "vv_done", "vv_one"))
        lg_mm, mx_done, nm_done, e_done, eT_mm, eT_done, pv_mm, rz_done, pv_done = (
            sem(s) for s in ("lg_mm", "mx_done", "nm_done", "e_done", "eT_mm", "eT_done", "pv_mm", "rz_done", "pv_done"))
        pT_mm, pT_hi, pT_lo, op_mm, x2_done = (sem(s) for s in ("pT_mm", "pT_hi", "pT_lo", "op_mm", "x2_done"))
        k_done, wg_hi_done, wg_lo_done, gl_mm, gT_done, gl2_mm, ge_done, g_step, gm_done = (
            sem(s) for s in ("k_done", "wg_hi_done", "wg_lo_done", "gl_mm", "gT_done", "gl2_mm", "ge_done", "g_step", "gm_done"))
        v_zero, v_mm, v_gated, v_added = (sem(s) for s in ("v_zero", "v_mm", "v_gated", "v_added"))
        og_done, oT_mm, oT_hi, oT_lo, out_mm, fin, st_out = (
            sem(s) for s in ("og_done", "oT_mm", "oT_hi", "oT_lo", "out_mm", "fin", "st_out"))

        block = ctx.enter_context(nc.Block())

        W_Q1, W_OUT, W_Q2, W_K2, W_VE, W_OE = 0, 1, 2, 3, 4, 4 + NE
        w_fixed = [a["qw"], a["owT"], a["wq2"], a["wk2"]]

        def blocks(w):
            return w.rearrange("(k p) n -> p k n", p=P)

        def half(h):
            return slice(4 * h, 4 * h + 4)

        def chunk(c):
            return (slice(ROWS * c, ROWS * c + ROWS), P) if c < CH else (slice(CH * ROWS, CH * ROWS + 1), REM)

        def gram_cols(m):
            return min(m, KC - 2) * P

        def pv_bank(u):
            return bank[4 + (u % 2 if u < H1 else u % 4)]

        def three(pe, dst, wh, wl, xh, xl, first, last):
            pe.matmul(dst, wh, xh, start=first, stop=False)
            pe.matmul(dst, wh, xl, start=False, stop=False)
            return pe.matmul(dst, wl, xh, start=False, stop=last)

        @block.sync
        def _(sp):
            sp.dma_start(xres[:, :, :], a["x"].rearrange("b s d -> (b s) d").rearrange("(i p) d -> p i d", p=P)).then_inc(ld_x, 16)
            sp.dma_start(mb[:, :, :], blocks(a["WqT"])).then_inc(ld_wq, 16)
            sp.dma_start(bq[:, :], a["bq"].rearrange("(k p) -> p k", p=P), allow_slow_non_contiguous=True).then_inc(ld_bq, 16)

            def load_ctx(b, c):
                r, k = chunk(c)
                if c < CH:
                    src = a["ctx_1024"][b, c * P * ROWS:(c + 1) * P * ROWS, :].rearrange("(p r) d -> p r d", r=ROWS)
                else:
                    src = a["ctx_1024"][b, CH * P * ROWS:T, :].rearrange("p (r d) -> p r d", r=1)
                sp.dma_start(raw[0:k, r, :], src).then_inc(ld_ctx[c], 16)

            for c in (3, 0, 1, 2):
                load_ctx(0, c)
            sp.dma_start(kv[:, 0:4, :], blocks(a["qw"])).then_inc(ld_qv, 16)
            sp.dma_start(kv[:, 4:8, :], blocks(a["vw"])).then_inc(ld_qv, 16)
            sp.dma_start(wv_raw, blocks(a["WvT"])).then_inc(ld_wv, 16)
            sp.dma_start(wk[:, :, :], blocks(a["WkT"])).then_inc(ld_wk, 16)
            for t, name in ((gamma, "gamma"), (beta, "beta"), (out_b, "out_b")):
                sp.dma_start(t[:, :], a[name].rearrange("(o d) -> o d", o=1).broadcast_to([P, D])).then_inc(ld_par, 16)
            sp.dma_start(bv8[:, :], a["bv"].rearrange("(o d) -> o d", o=1).broadcast_to([B, D])).then_inc(ld_par, 16)
            with sp.Fori(1, B) as b:
                for c in range(CH + 1):
                    sp.wait_ge(ctx_sum, b * NADD + (SUMMED[c] - NADD))
                    load_ctx(b, c)
            sp.wait_ge(gh_done, 5 * B)
            sp.wait_ge(gl_done, 5 * B)
            sp.wait_ge(gt_mm, B)
            sp.dma_start(g32[:, :, :], blocks(a["WvT"])).then_inc(ld_wv2, 16)
            sp.wait_ge(ctx_lo, 4 * B)
            sp.wait_ge(ctx_sum, NADD * B)
            row = lambda name: a[name].rearrange("(o d) -> o d", o=1).unsqueeze(1).broadcast_to([1, B, D])
            sp.dma_start(b2[0:1, :, :], row("bv")).then_inc(ld_bvrow, 16)
            sp.dma_start(raw[:, half(0), :], blocks(a["qw"])).then_inc(ld_w[0], 16)
            sp.wait_ge(s_mm, 1)
            sp.dma_start(a2[1:2, :, :], row("bk")).then_inc(ld_rows, 16)
            sp.wait_ge(rk_done, 1)
            sp.dma_start(a2[0:1, :, :], rk).then_inc(ld_rows, 16)
            sp.wait_ge(rv_done, 1)
            sp.dma_start(b2[1:2, :, :], rv).then_inc(ld_rows, 16)
            sp.wait_ge(r2_mm, B)
            sp.dma_start(raw[:, half(1), :], blocks(a["owT"])).then_inc(ld_w[1], 16)
            sp.wait_ge(wg_hi_done, 1)
            sp.dma_start(wg_raw[:, :, 0:H2 * NE], blocks(a["wg"])).then_inc(ld_wg, 16)
            sp.wait_ge(w_lo, 3)
            sp.dma_start(raw[:, half(0), :], blocks(a["wq2"])).then_inc(ld_w[0], 16)
            sp.wait_ge(w_lo, 4)
            sp.dma_start(raw[:, half(1), :], blocks(a["wk2"])).then_inc(ld_w[1], 16)
            for s in range(2):
                sp.wait_ge(w_lo, 5 + s)
                sp.dma_start(raw[:, half(s), :], blocks(a["ve"][s])).then_inc(ld_w[s], 16)
            with sp.Fori(1, NE // 2) as j:
                for s in range(2):
                    sp.wait_ge(w_lo, j * 2 + 5 + s)
                    sp.dma_start(raw[:, half(s), :], blocks(a["ve"][j * 2 + s])).then_inc(ld_w[s], 16)
            with sp.Fori(0, NE // 2) as j:
                for s in range(2):
                    sp.wait_ge(w_lo, j * 2 + 5 + NE + s)
                    sp.dma_start(raw[:, half(s), :], blocks(a["oe"][j * 2 + s])).then_inc(ld_w[s], 16)
            outv = out.rearrange("b s d -> (b s) d").rearrange("(i p) d -> p i d", p=P)
            for i in range(NT):
                sp.wait_ge(fin, i + 1)
                sp.dma_start(outv[:, i, :], xres[:, i, :]).then_inc(st_out, 16)
            sp.wait_ge(st_out, 16 * NT)

        @block.gpsimd
        def _(pool):
            pool.memset(ident[:, :], 0.0).then_inc(consts, 1)
            pool.memset(identb[:, :], 0.0).then_inc(consts, 1)
            pool.memset(headmask[:, :], 1.0).then_inc(consts, 1)
            pool.memset(posmask[:, :], MASKED).then_inc(consts, 1)
            pool.memset(causal[:, :], 0.0).then_inc(consts, 1)
            pool.memset(ones[:, :], 1.0).then_inc(consts, 1)
            pool.memset(expo[:, :], -0.5).then_inc(consts, 1)
            pool.memset(neghalf[:, :].bitcast(F32), -0.5).then_inc(consts, 1)
            tie4 = tie[:, :].rearrange("p (g e) -> p g e", e=NE)
            for e in range(NE):
                pool.memset(tie4[:, :, e], float(NE - e)).then_inc(consts, 1)
            pool.wait_ge(consts, 8 + NE)
            for m in (ident, identb):
                pool.affine_select(out=m[:, :], in_=m[:, :], compare_op=ALU.not_equal, fill=1.0, base=0,
                                   pattern=[[-1, P]], channel_multiplier=1).then_inc(consts, 1)
            hm = headmask[:, :].rearrange("p (h d) -> p h d", d=D1)
            pool.affine_select(out=hm, in_=hm, compare_op=ALU.is_ge, fill=0.0, base=0,
                               pattern=[[-D1, 4], [0, D1]], channel_multiplier=1).then_inc(consts, 1)
            pool.wait_ge(consts, 11 + NE)
            pool.affine_select(out=hm, in_=hm, compare_op=ALU.is_ge, fill=0.0, base=D1 - 1,
                               pattern=[[D1, 4], [0, D1]], channel_multiplier=-1).then_inc(consts, 1)

            def rstd_of(n, i):
                pool.wait_ge(s_var[n], i + 1)
                pool.tensor_tensor(rstd[:, i:i + 1], vareps[:, i:i + 1], expo[:, 0:1], ALU.pow).then_inc(s_rstd[n], 1)

            for i in range(NT):
                rstd_of(0, i)

            pm = posmask[:, :].rearrange("p (s q) -> p s q", q=16)
            for t in range(P // 16):
                for k in ((-1, 1) if t else (1,)):
                    n = 2 * t - (1 if k < 0 else 0)
                    if n:
                        pool.wait_ge(bfconst, n)
                    pool.affine_select(out=pm, in_=pm, compare_op=ALU.not_equal, fill=0.0, base=-16 * t * k,
                                       pattern=[[0, 4 * P // 16], [-1, 16]], channel_multiplier=1).then_inc(bfconst, 1)
            n0 = 2 * (P // 16) - 1
            cz = causal[:, :].rearrange("p (r b j) -> p r b j", r=4, b=2)
            pool.affine_select(out=cz[:, :, 1, :], in_=cz[:, :, 1, :], compare_op=ALU.is_ge, fill=MASKED, base=-S,
                               pattern=[[0, 4], [-1, S]], channel_multiplier=1).then_inc(bfconst, 1)
            pool.affine_select(out=cz[:, :, 0, :], in_=cz[:, :, 0, :], compare_op=ALU.is_ge, fill=MASKED, base=0,
                               pattern=[[0, 4], [-1, S]], channel_multiplier=1).then_inc(bfconst, 1)
            pool.wait_ge(bfconst, n0 + 2)
            pool.affine_select(out=cz[:, :, 0, :], in_=cz[:, :, 0, :], compare_op=ALU.is_ge, fill=MASKED, base=S - 1,
                               pattern=[[0, 4], [0, S]], channel_multiplier=-1).then_inc(bfconst, 1)

            pool.wait_ge(s_norm[0], NT)
            pool.wait_ge(ld_par, 64)
            for i in range(NT):
                pool.tensor_tensor(xres[:, i, :], xres[:, i, :], beta[:, :], ALU.add).then_inc(xb_done, 1)

            def sums(b, first):
                n = 0
                for t in range(1, NSLOT):
                    c, k = (t // ROWS, P) if t < CH * ROWS else (CH, REM)
                    if t % ROWS == 0 or t == 1:
                        pool.wait_ge(ld_ctx[c], b * 16 + 16)
                    if t > 1:
                        pool.wait_ge(ctx_sum, b * NADD + n)
                    elif not first:
                        pool.wait_ge(sum_out, b)
                    if t in SUMMED:
                        pool.wait_ge(ctx_lo, b * 4 + c + 1)
                    pool.tensor_tensor(psum_tmp[0:k, :], (raw[:, 0, :] if t == 1 else psum_tmp[0:k, :]), raw[0:k, t, :],
                                       ALU.add).then_inc(ctx_sum, 1)
                    n += 1

            sums(0, True)
            with pool.Fori(1, B) as b:
                sums(b, False)

            def mask_heads(b):
                pool.wait_ge(r2_tmp, b + 1)
                kvb = kv[:, b, :].rearrange("p (k n) -> p k n", n=P)
                pool.tensor_tensor(kvb, kvb, headmask[:, :].unsqueeze(1).broadcast_to([P, KC, P]), ALU.mult).then_inc(r2_even, 1)

            mask_heads(0)
            mask_heads(2)
            rstd_of(1, 0)
            mask_heads(4)
            rstd_of(2, 0)
            rstd_of(1, 1)
            mask_heads(6)
            rstd_of(1, 2)
            rstd_of(2, 1)
            rstd_of(1, 3)
            rstd_of(2, 2)
            rstd_of(2, 3)
            for i in range(NT):
                pool.wait_ge(s_norm[2], i + 1)
                pool.tensor_tensor(xres[:, i, :], xres[:, i, :], out_b[:, :], ALU.add).then_inc(ob_done, 1)
            pool.wait_ge(r2_mm, B)
            pool.memset(vv[:, :, :, D1:D1 + 1], 1.0).then_inc(vv_one, 1)
            pool.wait_ge(r2_mm, B)
            pool.wait_ge(ld_rows, 48)
            pool.memset(wg_raw[:, :, H2 * NE:P], 0.0).then_inc(wg_hi_done, 1)
            for i in range(NT):
                rstd_of(3, i)
            pool.wait_ge(pv_mm, H1)
            pool.memset(vals[:, :, :, :], 0.0).then_inc(v_zero, 1)
            pool.wait_ge(v_zero, 1)
            pool.memset(vals[:, :, :, D2:D2 + 1], 1.0).then_inc(v_zero, 1)

            def add_values(e):
                for i in range(NT):
                    pool.wait_ge(v_gated, e * NT + i + 1)
                    v = vals[:, i, :, 0:D2]
                    pool.tensor_tensor(v, v, tmp[:, i % 2, :].rearrange("p (h k) -> p h k", k=D2), ALU.add).then_inc(v_added, 1)

            with pool.Fori(0, NE) as e:
                add_values(e)

        @block.scalar
        def _(act):
            def xT_high(n):
                for k in range(KC):
                    act.wait_ge(xT_mm, KC * n + k + 1)
                    act.activation(gh[:, k, :], bank[k][:, :], ACT.Copy).then_inc(xT_hi, 1)

            act.wait_ge(ld_wq, 16)
            act.activation(wvh[:, :, :], mb[:, :, :], ACT.Copy).then_inc(w_hi, 1)
            xT_high(0)

            def ctx_high(b, c, first):
                r, k = chunk(c)
                act.wait_ge(ld_ctx[c], b * 16 + 16)
                if not first:
                    act.wait_ge(gram_mm, b * 4 + c - 3)
                act.activation(hi[0:k, r, :], raw[0:k, r, :], ACT.Copy).then_inc(ctx_hi, 1)

            def g_high(b, first):
                act.wait_ge(gram_mm, b * 4 + 4)
                if not first:
                    act.wait_ge(gl_done, b * 5)
                    act.wait_ge(gt_mm, b)
                act.activation(g32[:, 0, :], bank[0][:, :], ACT.Copy).then_inc(g_act, 1)
                act.activation(g32[:, 1, P:D], bank[1][:, P:D], ACT.Copy).then_inc(g_act, 1)

            def gh_high(b, first):
                if first:
                    act.wait_ge(q_mm, KC)
                else:
                    act.wait_ge(m_mm, b * 4)
                act.wait_ge(g_act, b * 2 + 2)
                act.wait_ge(g_dve, b + 1)
                act.activation(gh[:, 0, :], g32[:, 0, :], ACT.Copy).then_inc(gh_done, 1)
                act.activation(gh[:, 1, P:D], g32[:, 1, P:D], ACT.Copy).then_inc(gh_done, 1)
                act.activation(gh[:, 2:4, 2 * P:D], g32[:, 2:4, 2 * P:D], ACT.Copy).then_inc(gh_done, 1)
                act.wait_ge(gt_mm, b + 1)
                act.activation(gh[:, 1:4, 0:P], bank[3][:, 0:3 * P].rearrange("p (m n) -> p m n", n=P), ACT.Copy).then_inc(gh_done, 1)
                act.activation(gh[:, 2:4, P:2 * P], bank[4][:, 0:2 * P].rearrange("p (m n) -> p m n", n=P), ACT.Copy).then_inc(gh_done, 1)

            def m_copy(b):
                for m in range(KC):
                    act.wait_ge(m_mm, b * 4 + m + 1)
                    act.activation(mb[:, m, :], bank[5 + m % 2][:, :], ACT.Copy).then_inc(m_done, 1)

            ctx_high(0, 0, True)
            for c in range(1, 4):
                ctx_high(0, c, True)
            act.wait_ge(ld_wv, 16)
            act.wait_ge(q_mm, KC)
            act.activation(wvh[:, :, :], wv_raw, ACT.Copy).then_inc(w_hi, 1)
            ctx_high(1, 0, False)
            g_high(0, True)
            gh_high(0, True)
            with act.Fori(1, B - 1) as b:
                for c in range(1, 4):
                    ctx_high(b, c, False)
                g_high(b, False)
                ctx_high(b + 1, 0, False)
                m_copy(b - 1)
                gh_high(b, False)
            for c in range(1, 4):
                ctx_high(B - 1, c, False)
            g_high(B - 1, False)
            m_copy(B - 2)
            gh_high(B - 1, False)
            act.wait_ge(s_mm, 1)
            act.activation(scol[:, :, :], bank[0][:, 0:KC * B].rearrange("p (k b) -> p k b", b=B), ACT.Copy).then_inc(s_done, 1)
            m_copy(B - 1)
            act.wait_ge(r_mm, 1)
            act.activation(rk, bank[1][0:B, :], ACT.Copy).then_inc(rk_done, 1)

            def w_high(n, slot, count):
                act.wait_ge(ld_w[slot], 16 * count)
                act.activation(hi[:, half(slot), :], raw[:, half(slot), :], ACT.Copy).then_inc(w_hi, 1)

            w_high(W_Q1, 0, 1)
            w_high(W_OUT, 1, 1)
            xT_high(1)

            def regroup(t):
                return t.rearrange("p (g t q) -> p t g q", t=P // 16, q=16)

            for k in range(KC):
                act.wait_ge(q_mm, KC + k + 1)
                act.activation(regroup(qT[:, k, :]), bank[4 + k][:, :].rearrange("p (t g q) -> p t g q", g=NG, q=16),
                               ACT.Copy).then_inc(q_done, 1)
                act.activation(regroup(xn[:, k, :]), bank[4 + k][:, :].rearrange("p (t g q) -> p t g q", g=NG, q=16),
                               ACT.Square).then_inc(qq_done, 1)
                act.wait_ge(qq_done, k + 1)
                act.activation(wvh[:, k, :], xn[:, k, :], ACT.Copy).then_inc(qq_hi, 1)
            def exps(u, scale):
                act.wait_ge(nm_done, u + 1)
                if u >= 2:
                    act.wait_ge(eT_mm, u - 1)
                for s in range(4):
                    act.activation(ering[:, u % 2, s * P:(s + 1) * P], bank[u % 2][:, s * P:(s + 1) * P], ACT.Exp,
                                   bias=negmax[:, u % 2, s:s + 1], scale=scale).then_inc(e_done, 1)

            for u in range(H1):
                exps(u, 2.0 * INV1)
            w_high(W_Q2, 0, 2)
            for k in range(KC):
                act.wait_ge(pT_mm, k + 1)
                act.activation(wvh[:, k, :].rearrange("p (t g q) -> p g t q", g=NG, q=16),
                               bank[k][:, :].rearrange("p (g t q) -> p g t q", g=NG, q=16), ACT.Copy).then_inc(pT_hi, 1)
            act.wait_ge(op_mm, NT)
            w_high(W_K2, 1, 2)
            act.wait_ge(ld_wg, 16)
            act.wait_ge(wg_hi_done, 1)
            act.activation(wg_hi, wg_raw, ACT.Copy).then_inc(wg_hi_done, 1)
            xT_high(2)
            for k in range(KC):
                act.wait_ge(q_mm, 2 * KC + k + 1)
                act.activation(qT[:, k, :], bank[4 + k][:, :], ACT.Copy, scale=SCALE2).then_inc(q_done, 1)
            w_high(W_VE, 0, 3)
            act.wait_ge(gl_mm, 1)
            act.activation(gateT[0:H2 * NE, :], bank[4][0:H2 * NE, :], ACT.Copy).then_inc(gT_done, 1)
            act.wait_ge(gl2_mm, 1)
            act.activation(gates, bank[5][:, 0:NT * H2 * NE], ACT.Exp, scale=-1.0).then_inc(ge_done, 1)
            for u in range(H1, H1 + 8):
                exps(u, 1.0)
            w_high(W_VE + 1, 1, 3)

            def expert_high(slot, count, used):
                act.wait_ge(ld_w[slot], count)
                act.wait_ge(used[0], used[1])
                act.activation(hi[:, half(slot), :], raw[:, half(slot), :], ACT.Copy).then_inc(w_hi, 1)

            with act.Fori(1, NE // 2) as j:
                for s in range(2):
                    expert_high(s, j * 16 + 48, (v_mm, (j * 2 + s) * NT - 4))
            for s in range(2):
                expert_high(s, 16 * (3 + NE // 2), (v_mm, (NE - 1 + s) * NT))

            def oT_high(e, buf):
                for k in range(KC):
                    act.wait_ge(oT_mm, e * 4 + k + 1)
                    act.activation(buf[:, k, :], bank[4 + k][:, :], ACT.Copy).then_inc(oT_hi, 1)

            oT_high(0, wvh)
            oT_high(1, gh)
            with act.Fori(0, NE // 2 - 1) as j:
                e = j * 2 + 1
                for s, buf in ((0, wvh), (1, gh)):
                    act.wait_ge(out_mm, e + s)
                    act.wait_ge(ld_w[s], e * 8 + 120)
                    act.activation(hi[:, half(s), :], raw[:, half(s), :], ACT.Copy).then_inc(w_hi, 1)
                    oT_high(e + (s + 1), buf)

        @block.tensor
        def _(pe):
            def value_query_products():
                pe.wait_ge(ld_qv, 32)
                pe.wait_ge(q_done, KC)
                for c in range(KC):
                    for k in range(KC):
                        cols = slice(c * P, (c + 1) * P)
                        mm = pe.matmul(bank[7][:, cols], kv[:, k, cols], kv[:, 4 + k, cols], start=(k == 0), stop=(k == KC - 1))
                mm.then_inc(c_mm, 1)

            def transposes(n):
                for i in range(NT):
                    pe.wait_ge(s_norm[(0, 2, 3)[n]], i + 1)
                    for k in range(KC):
                        mm = pe.transpose(bank[k][:, i * P:(i + 1) * P], xn[:, i, k * P:(k + 1) * P], ident[:, :])
                        if i == NT - 1:
                            mm.then_inc(xT_mm, 1)

            def project(wh, wl, banks, n):
                for c in range(KC):
                    for k in range(KC):
                        if c == 0:
                            pe.wait_ge(xT_lo, KC * n + k + 1)
                        cols = slice(c * P, (c + 1) * P)
                        mm = three(pe, bank[banks + c][:, :], wh[:, k, cols], wl[:, k, cols],
                                   gh[:, k, :], gl[:, k, :], k == 0, k == KC - 1)
                    mm.then_inc(q_mm, 1)

            pe.wait_ge(consts, 12 + NE)
            transposes(0)
            pe.wait_ge(w_lo, 1)
            project(wvh, wvl, 4, 0)

            def gram(b, first):
                for c in range(CH + 1):
                    r, kk = chunk(c)
                    pe.wait_ge(ctx_lo, b * 4 + c + 1)
                    if c == 0 and not first:
                        pe.wait_ge(g_act, b * 2)
                        pe.wait_ge(g_dve, b)
                    for t in range(r.start, r.stop):
                        start, stop = t == 0, t == NSLOT - 1
                        for m in range(KC):
                            n0 = gram_cols(m)
                            dst = bank[m][:, n0:D] if m < 2 else bank[2][:, (m - 2) * 2 * P:(m - 1) * 2 * P]
                            rows = slice(m * P, (m + 1) * P)
                            wh, wl = hi[0:kk, t, rows], lo[0:kk, t, rows]
                            xh, xl = hi[0:kk, t, n0:D], lo[0:kk, t, n0:D]
                            pe.matmul(dst, wh, xh, start=start and m < 3, stop=False, skip_group_check=m > 1)
                            pe.matmul(dst, wh, xl, start=False, stop=False, skip_group_check=m > 1)
                            mm = pe.matmul(dst, wl, xh, start=False, stop=stop, skip_group_check=m > 1)
                    mm.then_inc(gram_mm, 1)

            def g_transposes(b, first):
                pe.wait_ge(g_act, b * 2 + 2)
                pe.wait_ge(g_dve, b + 1)
                if first:
                    pe.wait_ge(q_done, KC)
                else:
                    pe.wait_ge(gl_done, b * 5)
                for n in range(1, KC):
                    pe.transpose(bank[3][:, (n - 1) * P:n * P], g32[:, 0, n * P:(n + 1) * P], ident[:, :])
                for n in range(2, KC):
                    mm = pe.transpose(bank[4][:, (n - 2) * P:(n - 1) * P], g32[:, 1, n * P:(n + 1) * P], ident[:, :])
                mm.then_inc(gt_mm, 1)

            def kv_of(b, first, between):
                pe.wait_ge(gl_done, b * 5 + 5)
                if first:
                    pe.wait_ge(w_lo, 2)
                    pe.wait_ge(q_done, KC)
                    pe.wait_ge(ld_wk, 16)
                for m in range(KC):
                    if not (first and m < 2):
                        pe.wait_ge(m_done, b * 4 + m - 1)
                    for k in range(KC):
                        rows = slice(m * P, (m + 1) * P)
                        mm = three(pe, bank[5 + m % 2][:, :], gh[:, k, rows], gl[:, k, rows], wvh[:, k, :], wvl[:, k, :],
                                   k == 0, k == KC - 1)
                    mm.then_inc(m_mm, 1)
                between()
                pe.wait_ge(m_done, b * 4 + 4)
                if first:
                    pe.wait_ge(c_done, 1)
                else:
                    pe.wait_ge(kv_done, b)
                for c in range(KC):
                    for k in range(KC):
                        cols = slice(c * P, (c + 1) * P)
                        mm = pe.matmul(bank[7][:, cols], wk[:, k, cols], mb[:, k, cols], start=(k == 0), stop=(k == KC - 1))
                mm.then_inc(kv_mm, 1)

            gram(0, True)
            value_query_products()
            g_transposes(0, True)
            gram(1, False)
            kv_of(0, True, lambda: g_transposes(1, False))
            with pe.Fori(2, B) as b:
                gram(b, False)
                kv_of(b - 1, False, lambda: g_transposes(b, False))

            pe.wait_ge(sum_out, B)
            pe.wait_ge(g_act, 2 * B)
            for b in range(B):
                for k in range(KC):
                    mm = pe.matmul(bank[0][:, k * B + b:k * B + b + 1], sx[:, b, k * P:(k + 1) * P], ones[:, :], start=True, stop=True)
            mm.then_inc(s_mm, 1)
            pe.wait_ge(s_done, 1)

            def sum_rows(n, w):
                for k in range(KC):
                    mm = pe.matmul(bank[n][0:B, :], scol[:, k, :], w[:, k, :], start=(k == 0), stop=(k == KC - 1))
                mm.then_inc(r_mm, 1)

            def v_rows():
                pe.wait_ge(g_dve, B)
                pe.wait_ge(ld_wv2, 16)
                sum_rows(2, g32)

            sum_rows(1, wk)
            kv_of(B - 1, False, v_rows)

            def rank2(b):
                if b == 0:
                    pe.wait_ge(ld_rows, 48)
                    pe.wait_ge(ld_bvrow, 16)
                if b >= 2:
                    pe.wait_ge(r2_tmp, b - 1)
                for c in range(KC):
                    cols = slice(c * P, (c + 1) * P)
                    mm = pe.matmul(bank[3 + b % 2][:, cols], a2[:, b, cols], b2[:, b, cols], start=True, stop=True)
                mm.then_inc(r2_mm, 1)

            def attend(i):
                if i == 2:
                    pe.wait_ge(kv_done, B)
                pe.wait_ge(r2_even, i + 1)
                pe.wait_ge(r2_done, i + 1)
                for b in (2 * i, 2 * i + 1):
                    for c in range(KC):
                        cols = slice(c * P, (c + 1) * P)
                        p0 = S * (b % 2)
                        mm = pe.matmul(bank[(5, 6, 7, 4)[i]][p0:p0 + S, cols], qT[:, c, b * S:(b + 1) * S], kv[:, b, cols],
                                       start=True, stop=True)
                mm.then_inc(att_mm, 1)

            for b in range(B):
                rank2(b)
                if b >= 3 and b % 2:
                    attend((b - 3) // 2)
            attend(NT - 1)

            transposes(1)
            pe.wait_ge(w_lo, 3)
            project(hi[:, half(0), :], lo[:, half(0), :], 4, 1)
            for g in range(NG):
                for c in range(KC):
                    pe.wait_ge(q_done, KC + c + 1)
                    mm = pe.matmul(bank[g][:, c * P:(c + 1) * P], qT[:, c, g * P:(g + 1) * P], cb[:, c, :], start=True, stop=True)
                mm.then_inc(vv_mm, 1)

            def logits_1(u):
                c, j = u // 4, slice(D1 * (u % 4), D1 * (u % 4) + D1)
                s = bank[u % 2]
                if u == 0:
                    pe.wait_ge(bfconst, 2 * (P // 16) + 2)
                    pe.wait_ge(vv_done, NG)
                if u < 2 or u % 4 == 0:
                    pe.wait_ge(qq_lo, c + 1)
                if u >= 2:
                    pe.wait_ge(e_done, 4 * (u - 1))
                pe.matmul(s[:, :], identb[:, :], posmask[:, :], start=True, stop=False)
                pe.matmul(s[:, :], neghalf[j, :], wvh[j, c, :], start=False, stop=False)
                pe.matmul(s[:, :], neghalf[j, :], wvl[j, c, :], start=False, stop=False)
                for g in range(NG):
                    q = qT[j, c, g * P:(g + 1) * P]
                    mm = pe.matmul(s[:, g * P:(g + 1) * P], q, q, start=False, stop=(g == NG - 1))
                mm.then_inc(lg_mm, 1)

            def transpose_e(u):
                pe.wait_ge(e_done, 4 * (u + 1))
                if u >= 2:
                    pe.wait_ge(eT_done, u - 1)
                for s in range(4):
                    mm = pe.transpose(bank[2 + u % 2][:, s * P:(s + 1) * P], ering[:, u % 2, s * P:(s + 1) * P], ident[:, :])
                mm.then_inc(eT_mm, 1)

            def weigh(u, eT, values, d):
                pe.wait_ge(eT_done, min(u, H1 + 7) + 1)
                if 2 <= u < H1:
                    pe.wait_ge(pv_done, u - 1)
                elif u >= H1 + 4:
                    pe.wait_ge(pv_done, u - 3)
                for s in range(4):
                    mm = pe.matmul(pv_bank(u)[:, s * (d + 1):(s + 1) * (d + 1)], eT[:, s * P:(s + 1) * P], values(s),
                                   start=True, stop=True)
                mm.then_inc(pv_mm, 1)

            for u in range(H1 + 2):
                if u < H1:
                    logits_1(u)
                if 1 <= u <= H1:
                    transpose_e(u - 1)
                if u >= 2:
                    h = u - 2
                    if h == 0:
                        pe.wait_ge(vv_one, 1)
                    weigh(h, kv[:, h % 2, :], lambda s: vv[:, s, h, :], D1)
            pe.wait_ge(pv_done, H1)
            for k in range(KC):
                for g in range(NG):
                    mm = pe.transpose(bank[k][:, g * P:(g + 1) * P], mb[:, g, k * P:(k + 1) * P], ident[:, :])
                mm.then_inc(pT_mm, 1)
            for i in range(NT):
                for k in range(KC):
                    if i == 0:
                        pe.wait_ge(pT_lo, k + 1)
                        pe.wait_ge(w_lo, 4)
                    rows = slice(i * P, (i + 1) * P)
                    mm = three(pe, bank[4 + i][:, :], wvh[:, k, rows], wvl[:, k, rows], hi[:, 4 + k, :], lo[:, 4 + k, :],
                               k == 0, k == KC - 1)
                mm.then_inc(op_mm, 1)

            pe.wait_ge(pT_lo, KC)
            transposes(2)
            pe.wait_ge(w_lo, 5)
            project(hi[:, half(0), :], lo[:, half(0), :], 4, 2)
            pe.wait_ge(w_lo, 6)
            project(hi[:, half(1), :], lo[:, half(1), :], 0, 2)
            pe.wait_ge(wg_lo_done, 1)
            pe.wait_ge(q_done, 2 * KC + 4)
            for k in range(KC):
                mm = three(pe, bank[4][:, :], wg_hi[:, k, :], wg_lo[:, k, :], gh[:, k, :], gl[:, k, :], k == 0, k == KC - 1)
            mm.then_inc(gl_mm, 1)
            pe.wait_ge(gT_done, 1)
            ne = H2 * NE
            for i in range(NT):
                mm = pe.transpose(bank[5][:, i * ne:(i + 1) * ne], gateT[0:ne, i * P:(i + 1) * P], ident[0:ne, 0:ne])
            mm.then_inc(gl2_mm, 1)

            def logits_2(u):
                i, hh = (u - H1) // 2, (u - H1) % 2
                s = bank[u % 2]
                if u == H1:
                    pe.wait_ge(k_done, KC)
                if u >= H1 + 2:
                    pe.wait_ge(e_done, 4 * (u - 1))
                pe.matmul(s[:, :], identb[:, :], causal[:, :], start=True, stop=False)
                for n in range(4):
                    h = 2 * n + hh
                    j, c, rows = slice(D2 * (h % 2), D2 * (h % 2) + D2), h // 2, slice(i * P, (i + 1) * P)
                    mm = pe.matmul(s[:, n * P:(n + 1) * P], qT[j, c, rows], mb[j, c, rows], start=False, stop=(n == 3))
                mm.then_inc(lg_mm, 1)

            for u in range(H1, H1 + 9):
                if u < H1 + 8:
                    logits_2(u)
                if u > H1:
                    transpose_e(u - 1)

            def value_products(e, slot, first):
                pe.wait_ge(w_lo, e + 7)
                for i in range(NT):
                    if first:
                        pe.wait_ge(ge_done, 1)
                    else:
                        pe.wait_ge(v_gated, e * NT + i - 3)
                    for k in range(KC):
                        rows = slice(i * P, (i + 1) * P)
                        mm = three(pe, bank[4 + i][:, :], gh[:, k, rows], gl[:, k, rows], hi[:, 4 * slot + k, :],
                                   lo[:, 4 * slot + k, :], k == 0, k == KC - 1)
                    mm.then_inc(v_mm, 1)

            value_products(0, 0, True)
            with pe.Fori(0, NE // 2 - 1) as j:
                e = j * 2 + 1
                value_products(e, 1, False)
                value_products(e + 1, 0, False)
            value_products(NE - 1, 1, False)
            pe.wait_ge(v_zero, 2)
            for u in range(H1, H1 + 8):
                i, hh = (u - H1) // 2, (u - H1) % 2
                if u < H1 + 4:
                    pe.wait_ge(v_added, (NE - 1) * NT + u - H1 + 1)
                weigh(u, kv[:, u - H1, :], lambda s: vals[:, i, 2 * s + hh, :], D2)

            def gated_T(e):
                pe.wait_ge(og_done, e * NT + NT)
                for k in range(KC):
                    if not isinstance(e, int) or e:
                        pe.wait_ge(oT_lo, e * 4 + k - 3)
                    for i in range(NT):
                        mm = pe.transpose(bank[4 + k][:, i * P:(i + 1) * P], xn[:, i, k * P:(k + 1) * P], ident[:, :])
                    mm.then_inc(oT_mm, 1)

            def output_products(e, slot, bh, bl, first, last, between=lambda: None):
                pe.wait_ge(w_lo, e + (7 + NE))
                for i in range(NT):
                    if i == 2:
                        between()
                    for k in range(KC):
                        if i == 0:
                            pe.wait_ge(oT_lo, e * 4 + k + 1)
                        rows = slice(i * P, (i + 1) * P)
                        mm = three(pe, bank[i][:, :], bh[:, k, rows], bl[:, k, rows], hi[:, 4 * slot + k, :],
                                   lo[:, 4 * slot + k, :], first and k == 0, last and k == KC - 1)
                    if last:
                        mm.then_inc(out_mm, 1)
                if not last:
                    mm.then_inc(out_mm, 1)

            gated_T(0)
            output_products(0, 0, wvh, wvl, True, False, lambda: gated_T(1))
            with pe.Fori(0, NE // 2 - 1) as j:
                e = j * 2 + 1
                gated_T(e + 1)
                output_products(e, 1, gh, gl, False, False)
                gated_T(e + 2)
                output_products(e + 1, 0, wvh, wvl, False, False)
            output_products(NE - 1, 1, gh, gl, False, True)

        @block.vector
        def _(dve):
            def norm_front(n, i):
                src = xn if n == 1 else xres
                dve.bn_stats(stats[:, i, :], src[:, i, :]).then_inc(s_stats[n], 1)
                dve.wait_ge(s_stats[n], i + 1)
                dve.bn_aggr(mv[:, i, :], stats[:, i, :]).then_inc(s_aggr[n], 1)
                dve.wait_ge(s_aggr[n], i + 1)
                dve.tensor_scalar(vareps[:, i:i + 1], mv[:, i, 1:2], LN_EPS, None, ALU.add).then_inc(s_var[n], 1)

            def norm_back(n, i):
                src = xn if n == 1 else xres
                dve.wait_ge(s_rstd[n], i + 1)
                dve.tensor_scalar(xn[:, i, :], src[:, i, :], mv[:, i, 0:1], rstd[:, i:i + 1],
                                  ALU.subtract, ALU.mult).then_inc(s_norm[n], 1)

            def xT_low(n):
                for k in range(KC):
                    dve.wait_ge(xT_hi, KC * n + k + 1)
                    dve.tensor_tensor(gl[:, k, :], bank[k][:, :], gh[:, k, :].bitcast(F32), ALU.subtract).then_inc(xT_lo, 1)

            dve.wait_ge(ld_x, 16)
            for i in range(NT):
                norm_front(0, i)
            for i in range(NT):
                norm_back(0, i)
            dve.wait_ge(w_hi, 1)
            dve.tensor_tensor(wvl[:, :, :], mb[:, :, :], wvh[:, :, :].bitcast(F32), ALU.subtract).then_inc(w_lo, 1)
            xT_low(0)
            dve.wait_ge(ld_bq, 16)

            def query_copy(k):
                dve.wait_ge(q_mm, k + 1)
                dve.tensor_scalar(qT[:, k, :], bank[4 + k][:, :], bq[:, k:k + 1], INV1, ALU.add, ALU.mult).then_inc(q_done, 1)

            def ctx_low(b, c):
                r, k = chunk(c)
                dve.wait_ge(ctx_hi, b * 4 + c + 1)
                dve.tensor_tensor(lo[0:k, r, :], raw[0:k, r, :], hi[0:k, r, :].bitcast(F32), ALU.subtract).then_inc(ctx_lo, 1)

            def g_copy(b, first):
                dve.wait_ge(gram_mm, b * 4 + 4)
                if not first:
                    dve.wait_ge(gh_done, b * 5)
                    dve.wait_ge(gt_mm, b)
                dve.tensor_copy(g32[:, 2:4, 2 * P:D], bank[2][:, :].rearrange("p (m n) -> p m n", m=2)).then_inc(g_dve, 1)

            def gl_low(b):
                def sub(o, i0, i1):
                    dve.tensor_tensor(o, i0, i1.bitcast(F32), ALU.subtract).then_inc(gl_done, 1)
                dve.wait_ge(gh_done, b * 5 + 3)
                dve.wait_ge(g_dve, b + 1)
                sub(gl[:, 0, :], g32[:, 0, :], gh[:, 0, :])
                sub(gl[:, 1, P:D], g32[:, 1, P:D], gh[:, 1, P:D])
                sub(gl[:, 2:4, 2 * P:D], g32[:, 2:4, 2 * P:D], gh[:, 2:4, 2 * P:D])
                dve.wait_ge(gh_done, b * 5 + 5)
                sub(gl[:, 1:4, 0:P], bank[3][:, 0:3 * P].rearrange("p (m n) -> p m n", n=P), gh[:, 1:4, 0:P])
                sub(gl[:, 2:4, P:2 * P], bank[4][:, 0:2 * P].rearrange("p (m n) -> p m n", n=P), gh[:, 2:4, P:2 * P])

            def kv_copy(b):
                dve.wait_ge(kv_mm, b + 1)
                dve.tensor_copy(kv[:, b, :], bank[7][:, :]).then_inc(kv_done, 1)

            def sum_copy(b):
                dve.wait_ge(ctx_sum, b * NADD + NADD)
                dve.tensor_scalar(sx[:, b, :], psum_tmp[:, :], 1.0, None, ALU.mult).then_inc(sum_out, 1)

            for c in range(4):
                ctx_low(0, c)
                query_copy(c)
            dve.wait_ge(w_hi, 2)
            dve.tensor_tensor(wvl[:, :, :], wv_raw, wvh[:, :, :].bitcast(F32), ALU.subtract).then_inc(w_lo, 1)
            ctx_low(1, 0)
            g_copy(0, True)
            sum_copy(0)
            gl_low(0)
            dve.wait_ge(c_mm, 1)
            dve.wait_ge(consts, 12 + NE)
            dve.scalar_tensor_tensor(out=cb[:, :, :], in0=bank[7][:, :].rearrange("p (k n) -> p k n", n=P), scalar=INV1,
                                     in1=headmask[:, :].unsqueeze(1).broadcast_to([P, KC, P]),
                                     op0=ALU.mult, op1=ALU.mult).then_inc(c_done, 1)
            with dve.Fori(1, B - 1) as b:
                for c in range(1, 4):
                    ctx_low(b, c)
                g_copy(b, False)
                sum_copy(b)
                ctx_low(b + 1, 0)
                kv_copy(b - 1)
                gl_low(b)
            for c in range(1, 4):
                ctx_low(B - 1, c)
            g_copy(B - 1, False)
            sum_copy(B - 1)
            kv_copy(B - 2)
            gl_low(B - 1)
            dve.wait_ge(r_mm, 2)
            dve.scalar_tensor_tensor(out=rv, in0=bv8[:, :], scalar=float(T), in1=bank[2][0:B, :],
                                     op0=ALU.mult, op1=ALU.add).then_inc(rv_done, 1)

            def w_low(n, slot):
                dve.wait_ge(w_hi, n + 3)
                dve.tensor_tensor(lo[:, half(slot), :], raw[:, half(slot), :], hi[:, half(slot), :].bitcast(F32),
                                  ALU.subtract).then_inc(w_lo, 1)

            w_low(W_Q1, 0)
            kv_copy(B - 1)

            def rank2_add(b):
                dve.wait_ge(r2_mm, b + 1)
                dve.wait_ge(kv_done, b + 1)
                dve.tensor_tensor(kv[:, b, :], kv[:, b, :], bank[3 + b % 2][:, :], ALU.add).then_inc(r2_tmp, 1)
                if b % 2:
                    dve.wait_ge(r2_tmp, b + 1)
                    kvb = kv[:, b, :].rearrange("p (k n) -> p k n", n=P)
                    dve.tensor_tensor(kvb, kvb, headmask[:, :].unsqueeze(1).broadcast_to([P, KC, P]), ALU.mult).then_inc(r2_done, 1)

            def part1_out(i):
                dve.wait_ge(s_norm[0], i + 1)
                dve.wait_ge(att_mm, i + 1)
                dve.tensor_tensor(xn[:, i, :], xn[:, i, :], bank[(5, 6, 7, 4)[i]][:, :], ALU.add).then_inc(y_done, 1)
                dve.wait_ge(y_done, i + 1)
                norm_front(1, i)

            def part1_residual(i):
                norm_back(1, i)
                dve.wait_ge(s_norm[1], i + 1)
                dve.tensor_tensor(mb[:, i, :], xn[:, i, :], gamma[:, :], ALU.mult).then_inc(z_done, 1)
                dve.wait_ge(z_done, i + 1)
                dve.wait_ge(xb_done, i + 1)
                dve.tensor_tensor(xres[:, i, :], xres[:, i, :], mb[:, i, :], ALU.add).then_inc(x1_done, 1)
                dve.wait_ge(x1_done, i + 1)
                norm_front(2, i)

            for b in range(4):
                rank2_add(b)
            part1_out(0)
            for b in range(4, 6):
                rank2_add(b)
            part1_residual(0)
            part1_out(1)
            for b in range(6, B):
                rank2_add(b)
            norm_back(2, 0)
            part1_out(2)
            part1_residual(1)
            part1_out(3)
            norm_back(2, 1)
            part1_residual(2)
            part1_residual(3)
            norm_back(2, 2)
            norm_back(2, 3)
            xT_low(1)
            for k in range(KC):
                dve.wait_ge(qq_hi, k + 1)
                dve.tensor_tensor(wvl[:, k, :], xn[:, k, :], wvh[:, k, :].bitcast(F32), ALU.subtract).then_inc(qq_lo, 1)
            for g in range(NG):
                dve.wait_ge(vv_mm, g + 1)
                dve.tensor_copy(vv[:, g, :, 0:D1], bank[g][:, :].rearrange("p (h e) -> p h e", e=D1)).then_inc(vv_done, 1)
            w_low(W_OUT, 1)

            def unit_max(u, scale):
                dve.wait_ge(lg_mm, u + 1)
                if u >= 2:
                    dve.wait_ge(e_done, 4 * (u - 1))
                blocks4 = bank[u % 2][:, :].rearrange("p (s n) -> p s n", n=P)
                dve.tensor_reduce(rz[:, u % 2, :], blocks4, AX_X, ALU.max).then_inc(mx_done, 1)
                dve.wait_ge(mx_done, u + 1)
                dve.tensor_scalar(negmax[:, u % 2, :], rz[:, u % 2, :], -scale, None, ALU.mult).then_inc(nm_done, 1)

            def unit_eT(u, dst):
                dve.wait_ge(eT_mm, u + 1)
                dve.tensor_copy(dst, bank[2 + u % 2][:, :]).then_inc(eT_done, 1)

            def unit_out(u, dst, d):
                dve.wait_ge(pv_mm, u + 1)
                o = pv_bank(u)[:, 0:4 * (d + 1)].rearrange("p (s e) -> p s e", e=d + 1)
                rzu = stats[:, :, u % 2]
                if u >= 2:
                    dve.wait_ge(pv_done, u - 1)
                dve.reciprocal(rzu, o[:, :, d]).then_inc(rz_done, 1)
                dve.wait_ge(rz_done, u + 1)
                dve.tensor_tensor(dst, o[:, :, 0:d], rzu.unsqueeze(2).broadcast_to([P, 4, d]), ALU.mult).then_inc(pv_done, 1)

            for u in range(H1 + 2):
                if u < H1:
                    unit_max(u, 2.0 * INV1)
                if 1 <= u <= H1:
                    if u >= 3:
                        dve.wait_ge(pv_mm, u - 2)
                    unit_eT(u - 1, kv[:, (u - 1) % 2, :])
                if u >= 2:
                    h = u - 2
                    unit_out(h, mb[:, :, h * D1:(h + 1) * D1], D1)
            w_low(W_Q2, 0)
            for k in range(KC):
                dve.wait_ge(pT_hi, k + 1)
                dve.tensor_tensor(wvl[:, k, :].rearrange("p (t g q) -> p g t q", g=NG, q=16),
                                  bank[k][:, :].rearrange("p (g t q) -> p g t q", g=NG, q=16),
                                  wvh[:, k, :].bitcast(F32).rearrange("p (t g q) -> p g t q", g=NG, q=16),
                                  ALU.subtract).then_inc(pT_lo, 1)
            for i in range(NT):
                dve.wait_ge(op_mm, i + 1)
                dve.wait_ge(ob_done, i + 1)
                dve.tensor_tensor(xres[:, i, :], xres[:, i, :], bank[4 + i][:, :], ALU.add).then_inc(x2_done, 1)
                dve.wait_ge(x2_done, i + 1)
                norm_front(3, i)
                if i >= 1:
                    norm_back(3, i - 1)
            norm_back(3, NT - 1)
            xT_low(2)
            w_low(W_K2, 1)
            dve.wait_ge(wg_hi_done, 2)
            dve.tensor_tensor(wg_lo, wg_raw, wg_hi.bitcast(F32), ALU.subtract).then_inc(wg_lo_done, 1)
            w_low(W_VE, 0)
            for k in range(KC):
                dve.wait_ge(q_mm, 3 * KC + k + 1)
                dve.tensor_copy(mb[:, k, :], bank[k][:, :]).then_inc(k_done, 1)

            step = [0]

            def link(ins):
                step[0] += 1
                ins.then_inc(g_step, 1)
                dve.wait_ge(g_step, step[0])

            def by_head(t):
                return t.rearrange("p (g e) -> p g e", e=NE)

            def gate_part(n):
                if n == 0:
                    dve.wait_ge(ge_done, 1)
                    link(dve.tensor_scalar(gates, gates, 1.0, None, ALU.add))
                    link(dve.reciprocal(gates, gates))
                if n == 1:
                    link(dve.tensor_reduce(gmax[:, :], by_head(gates), AX_X, ALU.max))
                    link(dve.tensor_tensor(by_head(gsel), by_head(gates), gmax[:, :].unsqueeze(2).broadcast_to([P, NT * H2, NE]), ALU.is_equal))
                if n == 2:
                    link(dve.tensor_tensor(gsel, gsel, tie[:, :], ALU.mult))
                    link(dve.tensor_reduce(gmax[:, :], by_head(gsel), AX_X, ALU.max))
                if n == 3:
                    link(dve.tensor_tensor(by_head(gsel), by_head(gsel), gmax[:, :].unsqueeze(2).broadcast_to([P, NT * H2, NE]), ALU.is_equal))
                    dve.tensor_tensor(gm, gsel, gates, ALU.mult).then_inc(gm_done, 1)

            for u in range(H1, H1 + 9):
                if u < H1 + 8:
                    unit_max(u, 1.0)
                if u > H1:
                    if u == H1 + 1:
                        dve.wait_ge(pv_mm, H1)
                    unit_eT(u - 1, kv[:, u - 1 - H1, :])
                if H1 + 2 <= u < H1 + 6:
                    gate_part(u - H1 - 2)
            w_low(W_VE + 1, 1)

            def gated(e, first):
                g3 = gm.rearrange("p (i h e) -> p i h e", i=NT, h=H2)
                for i in range(NT):
                    dve.wait_ge(v_mm, e * NT + i + 1)
                    if not (first and i < 2):
                        dve.wait_ge(v_added, e * NT + i - 1)
                    g = g3[:, i, :, bass.ds(e, 1)] if not isinstance(e, int) else g3[:, i, :, e:e + 1]
                    dve.tensor_tensor(tmp[:, i % 2, :].rearrange("p (h k) -> p h k", k=D2),
                                      bank[4 + i][:, :].rearrange("p (h k) -> p h k", k=D2),
                                      g.broadcast_to([P, H2, D2]), ALU.mult).then_inc(v_gated, 1)

            def expert_lo(slot, count):
                dve.wait_ge(w_hi, count)
                dve.tensor_tensor(lo[:, half(slot), :], raw[:, half(slot), :], hi[:, half(slot), :].bitcast(F32),
                                  ALU.subtract).then_inc(w_lo, 1)

            dve.wait_ge(gm_done, 1)
            gated(0, True)
            expert_lo(0, 9)
            with dve.Fori(0, NE // 2 - 1) as j:
                e = j * 2 + 1
                gated(e, False)
                expert_lo(1, e + 9)
                gated(e + 1, False)
                expert_lo(0, e + 10)
            gated(NE - 1, False)

            def oT_low(e, bufh, bufl):
                for k in range(KC):
                    dve.wait_ge(oT_hi, e * 4 + k + 1)
                    dve.tensor_tensor(bufl[:, k, :], bank[4 + k][:, :], bufh[:, k, :].bitcast(F32), ALU.subtract).then_inc(oT_lo, 1)

            def gate_tile(e, i):
                g3 = gm.rearrange("p (i h e) -> p i h e", i=NT, h=H2)
                g = g3[:, i, :, bass.ds(e, 1)] if not isinstance(e, int) else g3[:, i, :, e:e + 1]
                dve.tensor_tensor(xn[:, i, :].rearrange("p (h k) -> p h k", k=D2),
                                  mb[:, i, :].rearrange("p (h k) -> p h k", k=D2),
                                  g.broadcast_to([P, H2, D2]), ALU.mult).then_inc(og_done, 1)

            def gate_out(e):
                dve.wait_ge(oT_mm, e * 4)
                for i in range(NT):
                    gate_tile(e, i)

            for u in range(H1, H1 + 8):
                i, hh = (u - H1) // 2, (u - H1) % 2
                unit_out(u, mb[:, i, :].rearrange("p (s hh e) -> p s hh e", hh=2, e=D2)[:, :, hh, :], D2)
                if hh:
                    dve.wait_ge(pv_done, u + 1)
                    gate_tile(0, i)
            oT_low(0, wvh, wvl)
            gate_out(1)
            expert_lo(1, NE + 8)
            oT_low(1, gh, gl)
            with dve.Fori(0, NE // 2 - 1) as j:
                e = j * 2 + 1
                for s, bh, bl in ((0, wvh, wvl), (1, gh, gl)):
                    gate_out(e + (s + 1))
                    expert_lo(s, e + (16 + s))
                    oT_low(e + (s + 1), bh, bl)
            for i in range(NT):
                dve.wait_ge(out_mm, NE + i)
                dve.tensor_tensor(xres[:, i, :], xres[:, i, :], bank[i][:, :], ALU.add).then_inc(fin, 1)


def kernel(x, ctx_1024, L0_xattn_Wq, L0_xattn_bq, L0_xattn_Wk, L0_xattn_bk, L0_xattn_Wv, L0_xattn_bv,
           L0_xattn_ln_gamma, L0_xattn_ln_beta, L0_attn_q_weight, L0_attn_v_weight, L0_attn_out_w, L0_attn_out_b,
           L0_ffn_w_q, L0_ffn_w_k, L0_ffn_w_gate, L0_ffn_value_experts, L0_ffn_output_experts):
    import numpy as np
    import concourse.bacc as bacc
    from concourse.bass_utils import run_bass_kernel_spmd

    D = x.shape[-1]
    E = L0_ffn_value_experts.shape[0]
    host = {
        "x": x, "ctx_1024": ctx_1024,
        "WqT": L0_xattn_Wq.T, "WkT": L0_xattn_Wk.T, "WvT": L0_xattn_Wv.T,
        "bq": L0_xattn_bq, "bk": L0_xattn_bk, "bv": L0_xattn_bv,
        "gamma": L0_xattn_ln_gamma, "beta": L0_xattn_ln_beta,
        "qw": L0_attn_q_weight.reshape(D, D), "vw": L0_attn_v_weight.reshape(D, D),
        "owT": L0_attn_out_w.T, "out_b": L0_attn_out_b,
        "wq2": L0_ffn_w_q, "wk2": L0_ffn_w_k, "wg": L0_ffn_w_gate,
        "ve": L0_ffn_value_experts.transpose(0, 2, 1, 3).reshape(E, D, D),
        "oe": L0_ffn_output_experts.reshape(E, D, D),
    }
    nc = bacc.Bacc("TRN2", target_bir_lowering=False, num_devices=1)
    arrays, drams = {}, {}
    for name, v in host.items():
        v = np.ascontiguousarray(v)
        arrays[f"in_{name}"] = v
        drams[name] = nc.dram_tensor(f"in_{name}", v.shape, mybir.dt.from_np(v.dtype), kind="ExternalInput").ap()
    out = nc.dram_tensor("out", x.shape, F32, kind="ExternalOutput").ap()
    perceiver_block(nc, drams, out)
    r = run_bass_kernel_spmd(nc, [arrays], core_ids=[0])
    return r.results[0]["out"]
```
